# Optimizing a Trainium2 kernel written in Bass

```python
import numpy as np
import jax
import jax.numpy as jnp

def _softmax(x, axis=-1):
    return jax.nn.softmax(x, axis=axis)

def _gelu(x):
    return jax.nn.gelu(x, approximate=True)

def _silu(x):
    return jax.nn.silu(x)

def _sigmoid(x):
    return jax.nn.sigmoid(x)

def _layernorm(x, axis=-1, eps=1e-05):
    m = jnp.mean(x, axis=axis, keepdims=True)
    v = jnp.var(x, axis=axis, keepdims=True)
    return (x - m) / jnp.sqrt(v + eps)

def _scatter_add(tgt, idx, src, axis=0):
    return tgt.at[idx].add(src)

def _segment_sum(src, seg, n):
    return jax.ops.segment_sum(src, seg, n)
kernel_name = 'mk_pixart_resid_d1_seqx_r8_116e7c'

def setup_inputs(seed: int=0):
    np.random.seed(seed)
    _w = jnp.asarray

    def _rec_inputs():
        import jax
        import jax.numpy as jnp
        _rk = jax.random.key(seed)
        x = -0.0002928 + 1 * jax.random.normal(jax.random.fold_in(_rk, 1), (8, 128, 256), jnp.float32)
        _lenS = 128 - jax.random.randint(jax.random.fold_in(_rk, 7), (8,), 0, max(1, 128 // 4) + 1, jnp.int32)
        _lenS2 = 128 - jax.random.randint(jax.random.fold_in(_rk, 8), (8,), 0, max(1, 128 // 4) + 1, jnp.int32)
        _ctx_2048P = jax.random.normal(jax.random.fold_in(_rk, 11), (8, 16, 256), jnp.float32)
        _ctx_2048c = jax.random.dirichlet(jax.random.fold_in(_rk, 511), 0.3 * jnp.ones((16,), jnp.float32), (8, 128))
        _ctx_2048t = jnp.einsum('bsk,bkd->bsd', _ctx_2048c, _ctx_2048P)
        _ctx_2048t = _ctx_2048t * jax.lax.rsqrt(jnp.mean(jnp.square(_ctx_2048t)) + 1e-12) * 0.953939
        ctx_2048 = -1.39393e-06 + 0.999914 * (_ctx_2048t + 0.3 * jax.random.normal(jax.random.fold_in(_rk, 611), (8, 128, 256), jnp.float32))
        itok_B_779_1933 = jax.random.randint(jax.random.fold_in(_rk, 12), (8,), 779, 1934, jnp.int32)
        return (x, ctx_2048, itok_B_779_1933)
    x, ctx_2048, itok_B_779_1933 = _rec_inputs()

    def _L0_xcond_setup():
        import jax, jax.numpy as jnp
        import numpy as np
        NUM_HEADS = 8
        HEAD_DIM = 64
        AVG_K_LENGTH = 20
        SCALE = 1.0 / (HEAD_DIM ** 0.5 * float(np.log(AVG_K_LENGTH)))
        key = jax.random.key(seed)
        k1, k2, k3, k4 = jax.random.split(key, 4)
        B, HD, LQ, LK = (4, NUM_HEADS * HEAD_DIM, 256, 256)
        q = jax.random.normal(k1, (B, HD, LQ), dtype=jnp.float32)
        k = jax.random.normal(k2, (B, HD, LK), dtype=jnp.float32)
        v = jax.random.normal(k3, (B, HD, LK), dtype=jnp.float32)
        k_length = jax.random.randint(k4, (B,), 64, LK + 1, dtype=jnp.int32)
        return {'q': q, 'k': k, 'v': v, 'k_length': k_length}
    _L0_xcond_all = _L0_xcond_setup()
    _L0_xcond_in = {k: v for k, v in _L0_xcond_all.items() if k in ()}
    del _L0_xcond_all

    def _L0_ffn_setup():
        import jax, jax.numpy as jnp
        import numpy as np
        B, S, D = (4, 256, 256)
        E = 8
        H = 352
        CAP_F = 1.0

        def _moe(x, Wg, W1, W3, W2, sw1, sw3, sw2):
            b, sl, d = x.shape
            T = b * sl
            C = int(CAP_F * T / E)
            xt = x.reshape(T, d)
            probs = jax.nn.softmax(xt @ Wg, axis=-1)
            eidx = jnp.argmax(probs, axis=-1)
            gate = jnp.take_along_axis(probs, eidx[:, None], 1)[:, 0]
            oh = jax.nn.one_hot(eidx, E, dtype=jnp.int32)
            pos = (jnp.cumsum(oh, axis=0) * oh).sum(-1) - 1
            keep = pos < C
            flat = jnp.where(keep, eidx * C + pos, E * C)
            xd = jnp.zeros((E * C, d), x.dtype).at[flat].set(xt, mode='drop')
            xd = xd.reshape(E, C, d)
            h = jax.nn.silu(jnp.einsum('ecd,edh->ech', xd, W1)) * jnp.einsum('ecd,edh->ech', xd, W3)
            oe = jnp.einsum('ech,ehd->ecd', h, W2).reshape(E * C, d)
            out = jnp.take(oe, jnp.minimum(flat, E * C - 1), axis=0)
            out = out * (gate * keep.astype(x.dtype))[:, None]
            shared = jax.nn.silu(xt @ sw1) * (xt @ sw3) @ sw2
            return (out + shared).reshape(b, sl, d)
        key = jax.random.key(seed)
        ks = jax.random.split(key, 8)
        s = lambda fan: 1.0 / np.sqrt(fan)
        return {'x': jax.random.normal(ks[0], (B, S, D), jnp.float32), 'Wg': jax.random.normal(ks[1], (D, E), jnp.float32) * s(D), 'W1': jax.random.normal(ks[2], (E, D, H), jnp.float32) * s(D), 'W3': jax.random.normal(ks[3], (E, D, H), jnp.float32) * s(D), 'W2': jax.random.normal(ks[4], (E, H, D), jnp.float32) * s(H), 'sw1': jax.random.normal(ks[5], (D, H), jnp.float32) * s(D), 'sw3': jax.random.normal(ks[6], (D, H), jnp.float32) * s(D), 'sw2': jax.random.normal(ks[7], (H, D), jnp.float32) * s(H)}
    _L0_ffn_all = _L0_ffn_setup()
    _L0_ffn_in = {k: v for k, v in _L0_ffn_all.items() if k in ('Wg', 'W1', 'W3', 'W2', 'sw1', 'sw3', 'sw2')}
    del _L0_ffn_all
    return {'x': x, 'ctx_2048': ctx_2048, 'itok_B_779_1933': itok_B_779_1933, 'L0_ffn_Wg': _L0_ffn_in['Wg'], 'L0_ffn_W1': _L0_ffn_in['W1'], 'L0_ffn_W3': _L0_ffn_in['W3'], 'L0_ffn_W2': _L0_ffn_in['W2'], 'L0_ffn_sw1': _L0_ffn_in['sw1'], 'L0_ffn_sw3': _L0_ffn_in['sw3'], 'L0_ffn_sw2': _L0_ffn_in['sw2']}

def reference(x, ctx_2048, itok_B_779_1933, L0_ffn_Wg, L0_ffn_W1, L0_ffn_W3, L0_ffn_W2, L0_ffn_sw1, L0_ffn_sw3, L0_ffn_sw2):
    import jax
    import jax.numpy as jnp

    def _L0_xcond_ref(q, k, v, k_length):
        import jax, jax.numpy as jnp
        import numpy as np
        NUM_HEADS = 8
        HEAD_DIM = 64
        AVG_K_LENGTH = 20
        SCALE = 1.0 / (HEAD_DIM ** 0.5 * float(np.log(AVG_K_LENGTH)))
        b, hd, lq = q.shape
        lk = k.shape[-1]
        d = hd // NUM_HEADS
        qh = q.reshape(b, NUM_HEADS, d, lq)
        kh = k.reshape(b, NUM_HEADS, d, lk)
        vh = v.reshape(b, NUM_HEADS, d, lk)
        s = SCALE * jnp.log(k_length.astype(jnp.float32))[:, None, None, None]
        attn = jnp.einsum('bhdq,bhdk->bhqk', qh, kh)
        attn = jax.nn.softmax(s * attn, axis=-1)
        out = jnp.einsum('bhqk,bhdk->bhdq', attn, vh)
        return out.reshape(b, hd, lq)

    def _L0_ffn_ref(x, Wg, W1, W3, W2, sw1, sw3, sw2):
        import jax, jax.numpy as jnp
        import numpy as np
        B, S, D = (4, 256, 256)
        E = 8
        H = 352
        CAP_F = 1.0

        def _moe(x, Wg, W1, W3, W2, sw1, sw3, sw2):
            b, sl, d = x.shape
            T = b * sl
            C = int(CAP_F * T / E)
            xt = x.reshape(T, d)
            probs = jax.nn.softmax(xt @ Wg, axis=-1)
            eidx = jnp.argmax(probs, axis=-1)
            gate = jnp.take_along_axis(probs, eidx[:, None], 1)[:, 0]
            oh = jax.nn.one_hot(eidx, E, dtype=jnp.int32)
            pos = (jnp.cumsum(oh, axis=0) * oh).sum(-1) - 1
            keep = pos < C
            flat = jnp.where(keep, eidx * C + pos, E * C)
            xd = jnp.zeros((E * C, d), x.dtype).at[flat].set(xt, mode='drop')
            xd = xd.reshape(E, C, d)
            h = jax.nn.silu(jnp.einsum('ecd,edh->ech', xd, W1)) * jnp.einsum('ecd,edh->ech', xd, W3)
            oe = jnp.einsum('ech,ehd->ecd', h, W2).reshape(E * C, d)
            out = jnp.take(oe, jnp.minimum(flat, E * C - 1), axis=0)
            out = out * (gate * keep.astype(x.dtype))[:, None]
            shared = jax.nn.silu(xt @ sw1) * (xt @ sw3) @ sw2
            return (out + shared).reshape(b, sl, d)
        return _moe(x, Wg, W1, W3, W2, sw1, sw3, sw2)
    x = x + _L0_xcond_ref(_layernorm(x, axis=-1), ctx_2048, ctx_2048, itok_B_779_1933)
    x = x + _L0_ffn_ref(_layernorm(x, axis=-1), L0_ffn_Wg, L0_ffn_W1, L0_ffn_W3, L0_ffn_W2, L0_ffn_sw1, L0_ffn_sw3, L0_ffn_sw2)
    return x

_drawn_inputs = setup_inputs


def setup_inputs(seed=0):
    import zlib

    import numpy as np

    out = dict(_drawn_inputs(seed))
    spreads = {}
    factors = {}
    for name, (base, spread) in spreads.items():
        noise = np.random.default_rng([zlib.crc32(name.encode()), seed]).standard_normal(out[name].shape)
        drawn = base * np.exp(spread * noise) if base else spread * noise
        out[name] = jnp.asarray(drawn.astype(out[name].dtype))
    for name, factor in factors.items():
        out[name] = (out[name] * factor).astype(out[name].dtype)
    return out
```

```python
from contextlib import ExitStack

import concourse.bass as bass
import numpy as np
from concourse import mybir

F32 = mybir.dt.float32
F32R = mybir.dt.float32r
BF16 = mybir.dt.bfloat16
I32 = mybir.dt.int32
U32 = mybir.dt.uint32
ALU = mybir.AluOpType
ACT = mybir.ActivationFunctionType
AX_X = mybir.AxisListType.X

P = 128
B, D = 8, 256
H, HD = 8, 16
NH = B * H
NG = NH // 4
E, C, F = 8, 128, 352
DC = D // P
FC = 3
FL = F - 2 * P
SCALE = 1.0 / (64 ** 0.5 * float(np.log(20)))
EPS = 1e-5

PART = P * D
QUERY_PARTS = (0, 0, 0, 1, 1, 1, 2)
KEY_PARTS = (0, 1, 2, 0, 1, 2, 0)
SLOTS = len(QUERY_PARTS)
KA = SLOTS * HD
KT = KA + 3
TWO_ONES = float(np.array([0x3F803F80], np.uint32).view(np.float32)[0])
NSTACK = 4
LAG = 13
CHUNKS = ((0, 1), (1, 2), (2, B))

IDENT, TRI, SELV, SELS, ECOL = 0, P, 2 * P, 4 * P, 6 * P
CONST_COLS = 6 * P + B * E

WG = E
S1, S3, S2 = 0, DC * (F + WG), DC * (F + WG) + DC * F
SCOLS = S2 + FC * D
W1, W3, W2 = 0, DC * F, 2 * DC * F
WCOLS = W2 + FC * D
NW = 3

VALUE, OUT_HI, OUT_LO, PLACE, NORM, STATS, TRSTD, TNORM, TTURN, THI, TLOW = 2, 3, 3, 4, 5, 6, 7, 8, 9, 9, 10
AFTER = 12
SPLIT = 4

MROW = 1

ROUTE = {n: i + 1 for i, n in enumerate((
    "lmax", "ldif", "cand", "first", "oh", "lsum", "gate", "cum", "pos", "keep", "slot", "slot2",
    "send", "idx_s", "fetch", "idx_g", "gkeep"))}


def constants():
    c = np.zeros((P, CONST_COLS), np.float32)
    r = np.arange(P)
    c[r, IDENT + r] = 1.0
    c[:, TRI:TRI + P] = r[:, None] <= r[None, :]
    for g in range(2):
        for j in range(4):
            head = HD * (4 * g + j)
            for d in range(HD):
                c[32 * j + d, SELV + g * P + head + d] = 1.0
                c[32 * j + HD, SELS + g * P + head + d] = 1.0
    c[:, ECOL:] = np.tile(E - np.arange(E), B)[None, :]
    return c


def block_kernel(nc, x, ctx_in, lens, wg, w1, w3, w2, sw1, sw3, sw2, consts, out):
    with ExitStack() as es:
        def sb(name, shape, dt):
            return es.enter_context(nc.sbuf_tensor(name, shape, dt))

        def sem(name):
            return es.enter_context(nc.semaphore(name))

        q_dram = nc.dram_tensor("q_parts", [B, 3, HD, H, D], BF16, kind="Internal").ap()
        k_dram = nc.dram_tensor("k_parts", [B, 3, HD, H, D], BF16, kind="Internal").ap()
        xd_dram = nc.dram_tensor("expert_rows", [E * C, D], F32, kind="Internal").ap()
        oe_dram = nc.dram_tensor("expert_results", [E * C, D], F32, kind="Internal").ap()

        cst = sb("cst", [P, CONST_COLS], F32)
        identb = sb("identb", [P, P], BF16)
        trib = sb("trib", [P, P], BF16)
        onesb = sb("onesb", [P, P], BF16)
        selr = sb("selr", [P, 4 * P], F32R)
        xs = sb("xs", [P, B, D], F32)
        cs = sb("cs", [P, B, D], F32)
        qf = sb("qf", [P, B, D], F32)
        rk = sb("rk", [P, B, D], F32)
        qp = sb("qp", [P, B, 3, D], BF16)
        kp = sb("kp", [P, B, 3, D], BF16)
        qst = sb("qst", [P, NSTACK, H, D], BF16)
        kst = sb("kst", [P, NSTACK, H, D], BF16)
        vext = sb("vext", [P, B, 2, H, 2 * HD], F32)
        pt = sb("pt", [P, 2, 4, 2 * D], F32)
        st = sb("st", [P, B, 6], F32)
        mv = sb("mv", [P, B, 2], F32)
        lnv = sb("lnv", [P, B], F32)
        rstd = sb("rstd", [P, B], F32)
        rs = sb("rs", [P, B], F32)
        leni = sb("leni", [P, B], I32)
        lenf = sb("lenf", [P, B], F32)
        lnlen = sb("lnlen", [P, B], F32)
        epst = sb("epst", [P, 1], F32)
        nm = sb("nm", [P, 2, H * 2], F32)
        nmr = sb("nmr", [P, 2, H * 2], F32)
        nm3 = sb("nm3", [P, 2, 3, H * 2], BF16)
        mrow = sb("mrow", [3 * H * 2, 2, P], BF16)
        ohi = sb("ohi", [P, 2, 2 * D], F32R)
        olo = sb("olo", [P, 2, 2 * D], F32R)
        rinv = sb("rinv", [P, D], F32)
        att = sb("att", [P, 2, D], F32)
        st2 = sb("st2", [P, B, 6], F32)
        mv2 = sb("mv2", [P, B, 2], F32)
        lnv2 = sb("lnv2", [P, B], F32)
        rstd2 = sb("rstd2", [P, B], F32)
        x2 = rk
        xhi = sb("xhi", [P, B, DC, P], F32R)
        xlo = sb("xlo", [P, B, DC, P], F32R)
        shi = sb("shi", [P, SCOLS], F32R)
        slo = sb("slo", [P, SCOLS], F32R)
        wraw = sb("wraw", [P, NW, SCOLS], F32)
        sraw = wraw[:, 0, :]

        sig = cs[:, 0:4, :].rearrange("p b d -> p (b d)")[:, 0:2 * F].rearrange("p (n f) -> p n f", n=2)
        xdT = cs[:, 4:8, :].rearrange("p b (c t) -> p b c t", c=DC)
        hs = qst[:].bitcast(F32).rearrange("p n h d -> p (n h d)")[:, 0:B * FC * P].rearrange(
            "p (b f) -> p b f", b=B)
        he = qf[:, 0:4, :].rearrange("p b d -> p (b d)")[:, 0:2 * FC * P].rearrange("p (n f) -> p n f", n=2)
        hTe = qf[:, 4:8, :].rearrange("p b d -> p (b d)")[:, 0:2 * FC * P].rearrange("p (n f) -> p n f", n=2)
        xe = rk
        hThi = sb("hThi", [P, FC * P], F32R)
        hTlo = sb("hTlo", [P, FC * P], F32R)
        ye = kp[:].bitcast(F32).rearrange("p b t d -> p (b t d)")[:, 0:2 * D].rearrange("p (n d) -> p n d", n=2)
        gat = kp[:].bitcast(F32).rearrange("p b t d -> p (b t d)")[:, 2 * D:2 * D + B * D].rearrange(
            "p (b d) -> p b d", b=B)
        res = qp[:].bitcast(F32).rearrange("p b t d -> p (b t d)")[:, 0:B * D].rearrange("p (b d) -> p b d", b=B)
        zero = sb("zero", [P, D], F32)
        lg = sb("lg", [P, B, E], F32)
        lmax = sb("lmax", [P, B], F32)
        ldif = sb("ldif", [P, B, E], F32)
        lexp = sb("lexp", [P, B, E], F32)
        lsum = sb("lsum", [P, B], F32)
        gate = sb("gate", [P, B], F32)
        cand = sb("cand", [P, B, E], F32)
        first = sb("first", [P, B], F32)
        oh = sb("oh", [P, B, E], BF16)
        cum = sb("cum", [P, B, E], F32)
        pos = sb("pos", [P, B], F32)
        keep = sb("keep", [P, B], F32)
        slot = sb("slot", [P, B], F32)
        slot2 = sb("slot2", [P, B], F32)
        send = sb("send", [P, B], F32)
        gkeep = sb("gkeep", [P, B], F32)
        idx_s = sb("idx_s", [P, B], U32)
        fetch = sb("fetch", [P, B], F32)
        idx_g = sb("idx_g", [P, B], U32)

        bank = [es.enter_context(nc.psum_tensor(f"bank{i}", [P, 512], F32)) for i in range(8)]
        mx_bank, sc_bank, O, R, X = bank[0:3], bank[3:5], bank[5], bank[6], bank[7]
        u1_bank, u3_bank, ht_bank, y_bank = bank[0:2], bank[2:4], bank[4:6], bank[6:8]

        ld_cst, ld_len = sem("ld_cst"), sem("ld_len")
        ld_ctx = [sem(f"ld_ctx{i}") for i in range(len(CHUNKS))]
        ld_x = [sem(f"ld_x{i}") for i in range(len(CHUNKS))]
        ld_shared = sem("ld_shared")
        ld_w = [sem(f"ld_w{i}") for i in range(NW)]
        st_q = [sem(f"st_q{i}") for i in range(len(CHUNKS))]
        st_k = [sem(f"st_k{i}") for i in range(len(CHUNKS))]
        ld_st = [sem(f"ld_st{i}") for i in range(NSTACK)]
        ld_m = [sem(f"ld_m{i}") for i in range(2)]
        xd_zeroed, xd_sent, ld_xe = sem("xd_zeroed"), sem("xd_sent"), sem("ld_xe")
        oe_stored = [sem(f"oe_stored{i}") for i in range(2)]
        out_stored = sem("out_stored")
        gathered = [sem(f"gathered{b}") for b in range(B)]
        eps_set, ones_set, sones_set, zero_set, pad_set, hpad_set = (
            sem(s) for s in ("eps_set", "ones_set", "sones_set", "zero_set", "pad_set", "hpad_set"))
        cst_copied, len_f, len_ln = sem("cst_copied"), sem("len_f"), sem("len_ln")
        k_hi, k_rest, k_mid, k_lo = (sem(s) for s in ("k_hi", "k_rest", "k_mid", "k_lo"))
        q_hi, q_rest, q_mid, q_lo = (sem(s) for s in ("q_hi", "q_rest", "q_mid", "q_lo"))
        q_stats, q_mv, q_ln, q_rstd, q_rs, q_made = (
            sem(s) for s in ("q_stats", "q_mv", "q_ln", "q_rstd", "q_rs", "q_made"))
        v_turned, v_copied = sem("v_turned"), sem("v_copied")
        scored, maxed, nm_hi, nm_rest, nm_mid, nm_lo = (
            sem(s) for s in ("scored", "maxed", "nm_hi", "nm_rest", "nm_mid", "nm_lo"))
        nm_turned, nm_row = sem("nm_turned"), sem("nm_row")
        shifted, exped, valued = sem("shifted"), sem("exped"), sem("valued")
        o_hi, o_lo, placed, inverted, normed, added = (
            sem(s) for s in ("o_hi", "o_lo", "placed", "inverted", "normed", "added"))
        x_stats, x_mv, x_ln, x_rstd, x2_made = (sem(s) for s in ("x_stats", "x_mv", "x_ln", "x_rstd", "x2_made"))
        x_turned, x_hi, x_lo = sem("x_turned"), sem("x_hi"), sem("x_lo")
        s_hi, s_lo = sem("s_hi"), sem("s_lo")
        up_done, silu_done, lg_copied, h_made = (sem(s) for s in ("up_done", "silu_done", "lg_copied", "h_made"))
        route, route_exp, pos_done = sem("route"), sem("route_exp"), sem("pos_done")
        h_turned, h_hi, h_lo, down_done, shared_added = (
            sem(s) for s in ("h_turned", "h_hi", "h_lo", "down_done", "shared_added"))
        xe_turned, xe_copied, eh_turned, eh_copied, e_up, e_silu, e_h, e_down, e_copied = (
            sem(s) for s in ("xe_turned", "xe_copied", "eh_turned", "eh_copied", "e_up", "e_silu", "e_h",
                             "e_down", "e_copied"))
        finished = sem("finished")

        block = es.enter_context(nc.Block())

        def ring_pass(n, size):
            return n // size + 1

        chunk_of = [next(i for i, (a, z) in enumerate(CHUNKS) if a <= b < z) for b in range(B)]

        @block.sync
        def _(sp):
            for i, (a, z) in enumerate(CHUNKS):
                sp.dma_start(cs[:, a:z, :], ctx_in[a:z].rearrange("b p d -> p b d")).then_inc(ld_ctx[i], 16)
                sp.dma_start(xs[:, a:z, :], x[a:z].rearrange("b p d -> p b d")).then_inc(ld_x[i], 16)
                if i == 0:
                    sp.dma_start(leni[:], bass.AP(tensor=lens.tensor, offset=lens.offset,
                                                  ap=[[0, P], [1, B]])).then_inc(ld_len, 16)
                    sp.dma_start(cst[:], consts).then_inc(ld_cst, 16)

            def store(parts, dram, done, ready, i):
                a, z = CHUNKS[i]
                if z - a == 1:
                    for part in range(3):
                        sp.wait_ge(ready[part], i + 1)
                        sp.dma_start(
                            bass.AP(tensor=dram.tensor, offset=(a * 3 + part) * PART,
                                    ap=[[D, H], [H * D, HD], [1, D]]),
                            parts[:, a, part, :]).then_inc(done[i], 16)
                else:
                    sp.wait_ge(ready[2], i + 1)
                    for h in range(H):
                        sp.dma_start(
                            bass.AP(tensor=dram.tensor, offset=a * 3 * PART + h * D,
                                    ap=[[H * D, HD], [PART, 3 * (z - a)], [1, D]]),
                            parts[HD * h:HD * h + HD, a:z, :, :].rearrange("p b t d -> p (b t) d")
                        ).then_inc(done[i], 16)

            def load_stack(b):
                s, i = b % NSTACK, chunk_of[b]
                n = 3 if i < 2 else H
                if b >= NSTACK:
                    sp.wait_ge(shifted, H * (b - NSTACK + 1))
                sp.wait_ge(sones_set, 1 if b == 0 else 2)
                sp.wait_ge(st_k[i], 16 * n)
                base = b * 3 * PART
                row = H * D
                kd, qd = kst[:, s].rearrange("p h d -> p (h d)"), qst[:, s].rearrange("p h d -> p (h d)")
                sp.dma_start(kd[0:96, :], bass.AP(tensor=k_dram.tensor, offset=base,
                                                  ap=[[0, 2], [row, 48], [1, row]])).then_inc(ld_st[s], 16)
                sp.dma_start(kd[96:112, :], bass.AP(tensor=k_dram.tensor, offset=base,
                                                    ap=[[row, HD], [1, row]])).then_inc(ld_st[s], 16)
                sp.wait_ge(st_q[i], 16 * n)
                for part in range(2):
                    sp.dma_start(qd[48 * part:48 * part + 48, :],
                                 bass.AP(tensor=q_dram.tensor, offset=base + part * PART,
                                         ap=[[0, 3], [row, HD], [1, row]])).then_inc(ld_st[s], 16)
                sp.dma_start(qd[96:112, :], bass.AP(tensor=q_dram.tensor, offset=base + 2 * PART,
                                                    ap=[[row, HD], [1, row]])).then_inc(ld_st[s], 16)

            def load_maxima(b):
                sp.wait_ge(nm_row, b + 1)
                for t in range(3):
                    sp.dma_start(qst[KA + t:KA + t + 1, b % NSTACK].rearrange("p h (u c) -> p (h u) c", u=2),
                                 mrow[16 * t:16 * t + 16, b % 2, :]).then_inc(ld_m[b % 2], 16)

            def load_expert(e):
                n = e % NW
                if e == 0:
                    sp.wait_ge(s_lo, 1)
                if e >= NW:
                    sp.wait_ge(e_down, e - NW + 1)
                sp.dma_start(wraw[:, n, W1:W3].rearrange("p (c f) -> p c f", c=DC),
                             w1[e].rearrange("(c p) f -> p c f", p=P)).then_inc(ld_w[n], 16)
                sp.dma_start(wraw[:, n, W3:W2].rearrange("p (c f) -> p c f", c=DC),
                             w3[e].rearrange("(c p) f -> p c f", p=P)).then_inc(ld_w[n], 16)
                sp.dma_start(wraw[:, n, W2:W2 + 2 * D].rearrange("p (c d) -> p c d", c=2),
                             w2[e, 0:2 * P].rearrange("(c p) d -> p c d", p=P)).then_inc(ld_w[n], 16)
                sp.dma_start(wraw[0:FL, n, W2 + 2 * D:WCOLS], w2[e, 2 * P:F]).then_inc(ld_w[n], 16)

            kr, qr = (k_hi, k_mid, k_lo), (q_hi, q_mid, q_lo)
            for i in range(2):
                store(kp, k_dram, st_k, kr, i)
                store(qp, q_dram, st_q, qr, i)
                load_stack(i)
            s1 = sraw[:, S1:S3].rearrange("p (c f) -> p c f", c=DC)
            sp.dma_start(s1[:, :, 0:F], sw1.rearrange("(c p) f -> p c f", p=P)).then_inc(ld_shared, 16)
            sp.dma_start(s1[:, :, F:], wg.rearrange("(c p) f -> p c f", p=P)).then_inc(ld_shared, 16)
            sp.dma_start(sraw[:, S3:S2].rearrange("p (c f) -> p c f", c=DC),
                         sw3.rearrange("(c p) f -> p c f", p=P)).then_inc(ld_shared, 16)
            sp.dma_start(sraw[:, S2:S2 + 2 * D].rearrange("p (c d) -> p c d", c=2),
                         sw2[0:2 * P].rearrange("(c p) d -> p c d", p=P)).then_inc(ld_shared, 16)
            sp.wait_ge(pad_set, 1)
            sp.dma_start(sraw[0:FL, S2 + 2 * D:], sw2[2 * P:F]).then_inc(ld_shared, 16)
            store(kp, k_dram, st_k, kr, 2)
            store(qp, q_dram, st_q, qr, 2)
            load_stack(2)
            load_stack(3)
            load_maxima(0)
            load_maxima(1)
            for b in range(NSTACK, B):
                load_stack(b)
                load_maxima(b - 2)
            load_maxima(B - 2)
            load_maxima(B - 1)
            for e in range(NW):
                load_expert(e)
            sp.wait_ge(zero_set, 1)
            sp.dma_start(xd_dram.rearrange("(n p) d -> p n d", p=P),
                         zero[:].unsqueeze(1).broadcast_to([P, E, D])).then_inc(xd_zeroed, 16)
            sp.wait_ge(xd_sent, 16 * B)
            sp.dma_start(xe[:, :, :], xd_dram.rearrange("(n p) d -> p n d", p=P)).then_inc(ld_xe, 16)
            for e in range(E):
                sp.wait_ge(e_copied, e + 1)
                sp.dma_start(oe_dram[e * C:(e + 1) * C, :], ye[:, e % 2, :]).then_inc(oe_stored[e % 2], 16)
                if e + NW < E:
                    load_expert(e + NW)
            for b in range(B):
                sp.wait_ge(finished, b + 1)
                sp.dma_start(out[b], res[:, b, :]).then_inc(out_stored, 16)
            sp.wait_ge(out_stored, 16 * B)

        @block.gpsimd
        def _(pool):
            def ones_rows(first, last):
                n = kst[96:P, first:last].rearrange("p n h d -> p (n h d)").bitcast(F32)
                nc.gpsimd.memset(n, TWO_ONES).then_inc(sones_set, 1)

            nc.gpsimd.memset(epst[:], EPS).then_inc(eps_set, 1)
            pool.wait_ge(eps_set, 1)
            ones_rows(0, 1)
            pool.wait_ge(sones_set, 1)
            for i, (a, z) in enumerate(CHUNKS):
                pool.wait_ge(k_hi, i + 1)
                nc.gpsimd.tensor_tensor(rk[:, a:z, :], cs[:, a:z, :], kp[:, a:z, 0, :],
                                        ALU.subtract).then_inc(k_rest, 1)
                pool.wait_ge(k_mid, i + 1)
                nc.gpsimd.tensor_tensor(kp[:, a:z, 2, :], rk[:, a:z, :], kp[:, a:z, 1, :],
                                        ALU.subtract).then_inc(k_lo, 1)
                if i == 0:
                    pool.wait_ge(k_lo, 1)
                    ones_rows(1, NSTACK)
                    pool.wait_ge(sones_set, 2)
                if i == 1:
                    nc.gpsimd.memset(vext[:, :, :, :, HD:], 1.0).then_inc(ones_set, 1)
                    nc.gpsimd.memset(onesb[:], 1.0).then_inc(ones_set, 1)
                    pool.wait_ge(ones_set, 2)
                    nc.gpsimd.memset(sraw[FL:P, S2 + 2 * D:], 0.0).then_inc(pad_set, 1)
                    pool.wait_ge(pad_set, 1)
            nc.gpsimd.memset(zero[:], 0.0).then_inc(zero_set, 1)

            def split_maxima(b):
                n = b % 2
                pool.wait_ge(maxed, H * (b + 1))
                if b >= 2:
                    pool.wait_ge(nm_turned, b - 1)
                nc.gpsimd.tensor_copy(nm3[:, n, 0, :], nm[:, n, :]).then_inc(nm_hi, 1)
                pool.wait_ge(nm_hi, b + 1)
                nc.gpsimd.tensor_tensor(nmr[:, n, :], nm[:, n, :], nm3[:, n, 0, :], ALU.subtract).then_inc(nm_rest, 1)
                pool.wait_ge(nm_rest, b + 1)
                nc.gpsimd.tensor_copy(nm3[:, n, 1, :], nmr[:, n, :]).then_inc(nm_mid, 1)
                pool.wait_ge(nm_mid, b + 1)
                nc.gpsimd.tensor_tensor(nm3[:, n, 2, :], nmr[:, n, :], nm3[:, n, 1, :], ALU.subtract).then_inc(nm_lo, 1)

            def add_attention(b):
                pool.wait_ge(normed, b + 1)
                nc.gpsimd.tensor_tensor(xs[:, b, :], xs[:, b, :], att[:, b % 2, :], ALU.add).then_inc(added, 1)

            for b in range(B):
                split_maxima(b)
                if b == 1:
                    pool.wait_ge(s_hi, 1)
                    nc.gpsimd.tensor_tensor(slo[:], sraw, shi[:].bitcast(F32), ALU.subtract).then_inc(s_lo, 1)
                if b >= 2:
                    add_attention(b - 2)
            for b in range(B - 2, B):
                add_attention(b)

            pool.wait_ge(xd_zeroed, 16)
            pool.wait_ge(x2_made, B)
            pool.wait_ge(route, ROUTE["idx_s"])
            for b in range(B):
                nc.gpsimd.indirect_dma_start(
                    xd_dram, bass.IndirectOffsetOnAxis(ap=idx_s[:, b:b + 1], axis=0), x2[:, b, :], None,
                    bounds_check=E * C - 1, oob_is_err=False).then_inc(xd_sent, 16)
            pool.wait_ge(route, ROUTE["idx_g"])
            for i in range(2):
                pool.wait_ge(oe_stored[i], 16 * E // 2)
            for b in range(B):
                nc.gpsimd.indirect_dma_start(
                    gat[:, b, :], None, oe_dram, bass.IndirectOffsetOnAxis(ap=idx_g[:, b:b + 1], axis=0),
                    bounds_check=E * C - 1, oob_is_err=False).then_inc(gathered[b], 16)

        @block.vector
        def _(dve):
            dve.wait_ge(ld_cst, 16)
            nc.vector.tensor_copy(identb[:], cst[:, IDENT:IDENT + P]).then_inc(cst_copied, 1)
            nc.vector.tensor_copy(trib[:], cst[:, TRI:TRI + P]).then_inc(cst_copied, 1)
            nc.vector.tensor_copy(selr[:], cst[:, SELV:SELV + 4 * P]).then_inc(cst_copied, 1)
            dve.wait_ge(ld_len, 16)
            nc.vector.tensor_copy(lenf[:], leni[:]).then_inc(len_f, 1)

            def queries(i):
                a, z = CHUNKS[i]
                dve.wait_ge(ld_x[i], 16)
                for b in range(a, z):
                    nc.vector.bn_stats(st[:, b, :], xs[:, b, :]).then_inc(q_stats, 1)
                for b in range(a, z):
                    dve.wait_ge(q_stats, b + 1)
                    nc.vector.bn_aggr(mv[:, b, :], st[:, b, :]).then_inc(q_mv, 1)
                dve.wait_ge(q_rstd, i + 1)
                dve.wait_ge(len_ln, 1)
                nc.vector.scalar_tensor_tensor(rs[:, a:z], rstd[:, a:z], SCALE, lnlen[:, a:z],
                                               ALU.mult, ALU.mult).then_inc(q_rs, 1)
                dve.wait_ge(q_rs, i + 1)
                for b in range(a, z):
                    nc.vector.tensor_scalar(qf[:, b, :], xs[:, b, :], mv[:, b, 0:1], rs[:, b:b + 1],
                                            ALU.subtract, ALU.mult).then_inc(q_made, 1)

            def split_queries(i):
                a, z = CHUNKS[i]
                dve.wait_ge(q_hi, i + 1)
                nc.vector.tensor_tensor(qf[:, a:z, :], qf[:, a:z, :], qp[:, a:z, 0, :],
                                        ALU.subtract).then_inc(q_rest, 1)
                dve.wait_ge(q_mid, i + 1)
                nc.vector.tensor_tensor(qp[:, a:z, 2, :], qf[:, a:z, :], qp[:, a:z, 1, :],
                                        ALU.subtract).then_inc(q_lo, 1)

            for i in range(len(CHUNKS)):
                queries(i)
                split_queries(i)

            def maximum(n):
                b, h = divmod(n, H)
                dve.wait_ge(scored, n + 1)
                if h == 0 and b >= 2:
                    dve.wait_ge(nm_lo, b - 1)
                nc.vector.tensor_reduce(nm[:, b % 2, 2 * h:2 * h + 2],
                                        mx_bank[n % 3][:].rearrange("p (u c) -> p u c", u=2),
                                        AX_X, ALU.max, negate=True).then_inc(maxed, 1)

            def low_output(b):
                dve.wait_ge(o_hi, b + 1)
                nc.vector.tensor_tensor(olo[:, b % 2, :], O[:], ohi[:, b % 2, :].bitcast(F32),
                                        ALU.subtract).then_inc(o_lo, 1)

            def normalise(b):
                dve.wait_ge(placed, b + 1)
                if b >= 1:
                    dve.wait_ge(normed, b)
                nc.vector.reciprocal(rinv[:], R[:, D:]).then_inc(inverted, 1)
                dve.wait_ge(inverted, b + 1)
                if b >= 2:
                    dve.wait_ge(added, b - 1)
                nc.vector.tensor_tensor(att[:, b % 2, :], R[:, 0:D], rinv[:], ALU.mult).then_inc(normed, 1)

            def token_stats(b):
                dve.wait_ge(added, b + 1)
                nc.vector.bn_stats(st2[:, b, :], xs[:, b, :]).then_inc(x_stats, 1)
                dve.wait_ge(x_stats, b + 1)
                nc.vector.bn_aggr(mv2[:, b, :], st2[:, b, :]).then_inc(x_mv, 1)

            def token_norm(b):
                dve.wait_ge(x_rstd, b + 1)
                nc.vector.tensor_scalar(x2[:, b, :], xs[:, b, :], mv2[:, b, 0:1], rstd2[:, b:b + 1],
                                        ALU.subtract, ALU.mult).then_inc(x2_made, 1)

            def low_tokens(b):
                dve.wait_ge(x_hi, b + 1)
                nc.vector.tensor_tensor(xlo[:, b].rearrange("p c t -> p (c t)"), X[:, 0:D],
                                        xhi[:, b].rearrange("p c t -> p (c t)").bitcast(F32),
                                        ALU.subtract).then_inc(x_lo, 1)

            for s in range(NH + LAG + AFTER):
                if s < NH:
                    maximum(s)
                for offset, work in ((OUT_LO, low_output), (NORM, normalise), (STATS, token_stats),
                                     (TNORM, token_norm), (TLOW, low_tokens)):
                    b, rest = divmod(s - LAG - H + 1 - offset, H)
                    if rest == 0 and 0 <= b < B:
                        work(b)

            dve.wait_ge(shifted, NH)
            nc.vector.memset(hs[:, :, F:], 0.0).then_inc(hpad_set, 1)
            for b in range(B):
                dve.wait_ge(silu_done, b + 1)
                nc.vector.tensor_tensor(hs[:, b, 0:F], u3_bank[b % 2][:, 0:F], sig[:, b % 2, :],
                                        ALU.mult).then_inc(h_made, 1)

            def bc(t):
                return t[:].unsqueeze(2).broadcast_to([P, B, E])

            dve.wait_ge(lg_copied, B)
            nc.vector.tensor_reduce(lmax[:], lg[:], AX_X, ALU.max).then_inc(route, 1)
            dve.wait_ge(route, ROUTE["lmax"])
            nc.vector.tensor_tensor(ldif[:], lg[:], bc(lmax), ALU.subtract).then_inc(route, 1)
            dve.wait_ge(route, ROUTE["ldif"])
            nc.vector.scalar_tensor_tensor(
                cand[:].rearrange("p b e -> p (b e)"), ldif[:].rearrange("p b e -> p (b e)"), 0.0,
                cst[:, ECOL:ECOL + B * E], ALU.is_ge, ALU.mult).then_inc(route, 1)
            dve.wait_ge(route, ROUTE["cand"])
            nc.vector.tensor_reduce(first[:], cand[:], AX_X, ALU.max).then_inc(route, 1)
            dve.wait_ge(route, ROUTE["first"])
            nc.vector.tensor_tensor(oh[:], cand[:], bc(first), ALU.is_equal).then_inc(route, 1)
            dve.wait_ge(route_exp, 1)
            nc.vector.tensor_reduce(lsum[:], lexp[:], AX_X, ALU.add).then_inc(route, 1)
            dve.wait_ge(route, ROUTE["lsum"])
            nc.vector.reciprocal(gate[:], lsum[:]).then_inc(route, 1)
            dve.wait_ge(pos_done, 1)
            nc.vector.tensor_tensor(cum[:], u1_bank[0][:, 0:B * E].rearrange("p (b e) -> p b e", b=B),
                                    oh[:], ALU.mult).then_inc(route, 1)
            dve.wait_ge(route, ROUTE["cum"])
            nc.vector.tensor_reduce(pos[:], cum[:], AX_X, ALU.add).then_inc(route, 1)
            dve.wait_ge(route, ROUTE["pos"])
            nc.vector.tensor_scalar(keep[:], pos[:], float(C), None, ALU.is_le).then_inc(route, 1)
            nc.vector.scalar_tensor_tensor(slot[:], first[:], -float(C), pos[:], ALU.mult,
                                           ALU.add).then_inc(route, 1)
            dve.wait_ge(route, ROUTE["slot"])
            nc.vector.tensor_scalar(slot2[:], slot[:], float(E * C - 1), None, ALU.add).then_inc(route, 1)
            dve.wait_ge(route, ROUTE["slot2"])
            nc.vector.scalar_tensor_tensor(send[:], keep[:], -float(2 * E * C), slot2[:], ALU.mult,
                                           ALU.add).then_inc(route, 1)
            dve.wait_ge(route, ROUTE["send"])
            nc.vector.tensor_scalar(idx_s[:], send[:], float(2 * E * C), None, ALU.add).then_inc(route, 1)
            nc.vector.tensor_scalar(fetch[:], slot2[:], float(E * C - 1), None, ALU.min).then_inc(route, 1)
            dve.wait_ge(route, ROUTE["fetch"])
            nc.vector.tensor_copy(idx_g[:], fetch[:]).then_inc(route, 1)
            nc.vector.tensor_tensor(gkeep[:], gate[:], keep[:], ALU.mult).then_inc(route, 1)

            def shared_low(b):
                dve.wait_ge(h_hi, b + 1)
                nc.vector.tensor_tensor(hTlo[:], ht_bank[b % 2][:, 0:FC * P], hThi[:].bitcast(F32),
                                        ALU.subtract).then_inc(h_lo, 1)

            def shared_add(b):
                dve.wait_ge(down_done, b + 1)
                nc.vector.tensor_tensor(xs[:, b, :], y_bank[b % 2][:, 0:D], xs[:, b, :],
                                        ALU.add).then_inc(shared_added, 1)

            def expert_hidden(e):
                dve.wait_ge(e_silu, e + 1)
                if e >= 2:
                    dve.wait_ge(eh_turned, e - 1)
                nc.vector.tensor_tensor(he[:, e % 2, 0:F], u3_bank[e % 2][:, 0:F], sig[:, e % 2, :],
                                        ALU.mult).then_inc(e_h, 1)

            def expert_hT(e):
                dve.wait_ge(eh_turned, e + 1)
                if e >= 2:
                    dve.wait_ge(e_down, e - 1)
                nc.vector.tensor_copy(hTe[:, e % 2, :], ht_bank[e % 2][:, 0:FC * P]).then_inc(eh_copied, 1)

            for b in range(SPLIT):
                shared_low(b)
                shared_add(b)
            dve.wait_ge(q_lo, len(CHUNKS))
            nc.vector.memset(he[:, :, F:], 0.0).then_inc(hpad_set, 1)
            for e in range(E + 1):
                if e < E:
                    expert_hidden(e)
                if e >= 1:
                    expert_hT(e - 1)
            for b in range(SPLIT, B):
                shared_low(b)
                shared_add(b)
            dve.wait_ge(shared_added, B)
            dve.wait_ge(route, ROUTE["gkeep"])
            for b in range(B):
                dve.wait_ge(gathered[b], 16)
                nc.vector.scalar_tensor_tensor(res[:, b, :], gat[:, b, :], gkeep[:, b:b + 1], xs[:, b, :],
                                               ALU.mult, ALU.add).then_inc(finished, 1)

        @block.scalar
        def _(act):
            act.wait_ge(ld_ctx[0], 16)
            act.wait_ge(eps_set, 1)

            def split_keys(i):
                a, z = CHUNKS[i]
                act.wait_ge(ld_ctx[i], 16)
                nc.scalar.copy(kp[:, a:z, 0, :], cs[:, a:z, :]).then_inc(k_hi, 1)

            def mid_keys(i):
                a, z = CHUNKS[i]
                act.wait_ge(k_rest, i + 1)
                nc.scalar.copy(kp[:, a:z, 1, :], rk[:, a:z, :]).then_inc(k_mid, 1)

            def query_rstd(i):
                a, z = CHUNKS[i]
                act.wait_ge(q_mv, z)
                nc.scalar.activation(lnv[:, a:z], mv[:, a:z, 1], ACT.Ln, bias=epst[:, 0:1]).then_inc(q_ln, 1)
                act.wait_ge(q_ln, i + 1)
                nc.scalar.activation(rstd[:, a:z], lnv[:, a:z], ACT.Exp, scale=-0.5).then_inc(q_rstd, 1)

            def split_q(i):
                a, z = CHUNKS[i]
                act.wait_ge(q_made, z)
                nc.scalar.copy(qp[:, a:z, 0, :], qf[:, a:z, :]).then_inc(q_hi, 1)
                act.wait_ge(q_rest, i + 1)
                nc.scalar.copy(qp[:, a:z, 1, :], qf[:, a:z, :]).then_inc(q_mid, 1)

            def values(b):
                act.wait_ge(v_turned, b + 1)
                if b == 0:
                    act.wait_ge(ones_set, 1)
                nc.scalar.copy(vext[:, b, :, :, 0:HD],
                               X[:, 0:2 * P].rearrange("p (c h d) -> p c h d", c=2, h=H)).then_inc(v_copied, 1)

            split_keys(0)
            act.wait_ge(len_f, 1)
            nc.scalar.activation(lnlen[:], lenf[:], ACT.Ln).then_inc(len_ln, 1)
            query_rstd(0)
            mid_keys(0)
            split_q(0)
            for i in range(1, len(CHUNKS)):
                split_keys(i)
                query_rstd(i)
                mid_keys(i)
                split_q(i)
            for b in range(B):
                values(b)

            def maxima_rows(b):
                act.wait_ge(nm_turned, b + 1)
                if b >= 2:
                    act.wait_ge(ld_m[b % 2], 48 * (b // 2))
                nc.scalar.copy(mrow[:, b % 2, :], X[0:48, 0:P // 2].bitcast(BF16)).then_inc(nm_row, 1)

            def exponentials(n):
                g = n // 4
                act.wait_ge(shifted, n + 1)
                if g >= 2:
                    act.wait_ge(valued, g - 1)
                nc.scalar.activation(pt[:, g % 2, n % 4, :], sc_bank[n % 2][:], ACT.Exp).then_inc(exped, 1)

            def high_output(b):
                act.wait_ge(valued, 2 * b + 2)
                if b >= 2:
                    act.wait_ge(placed, b - 1)
                nc.scalar.copy(ohi[:, b % 2, :], O[:]).then_inc(o_hi, 1)

            def token_rstd(b):
                act.wait_ge(x_mv, b + 1)
                nc.scalar.activation(lnv2[:, b:b + 1], mv2[:, b, 1:2], ACT.Ln, bias=epst[:, 0:1]).then_inc(x_ln, 1)
                act.wait_ge(x_ln, b + 1)
                nc.scalar.activation(rstd2[:, b:b + 1], lnv2[:, b:b + 1], ACT.Exp, scale=-0.5).then_inc(x_rstd, 1)

            def high_tokens(b):
                act.wait_ge(x_turned, b + 1)
                nc.scalar.copy(xhi[:, b].rearrange("p c t -> p (c t)"), X[:, 0:D]).then_inc(x_hi, 1)

            for s in range(NH + LAG + AFTER):
                b, rest = divmod(s - H - MROW, H)
                if rest == 0 and 0 <= b < B:
                    maxima_rows(b)
                if 0 <= s - LAG < NH:
                    exponentials(s - LAG)
                for offset, work in ((OUT_HI, high_output), (TRSTD, token_rstd), (THI, high_tokens)):
                    b, rest = divmod(s - LAG - H + 1 - offset, H)
                    if rest == 0 and 0 <= b < B:
                        work(b)
                if s == 6:
                    act.wait_ge(ld_shared, 16 * 5)
                    nc.scalar.copy(shi[:], sraw).then_inc(s_hi, 1)

            for b in range(B):
                act.wait_ge(up_done, b + 1)
                if b >= 2:
                    act.wait_ge(h_made, b - 1)
                nc.scalar.activation(sig[:, b % 2, :], u1_bank[b % 2][:, 0:F], ACT.Silu).then_inc(silu_done, 1)
                nc.scalar.copy(lg[:, b, :], u1_bank[b % 2][:, F:F + E]).then_inc(lg_copied, 1)
            act.wait_ge(route, ROUTE["ldif"])
            nc.scalar.activation(lexp[:], ldif[:], ACT.Exp).then_inc(route_exp, 1)

            def shared_high(b):
                act.wait_ge(h_turned, b + 1)
                if b >= 1:
                    act.wait_ge(down_done, b)
                nc.scalar.copy(hThi[:], ht_bank[b % 2][:, 0:FC * P]).then_inc(h_hi, 1)

            for b in range(SPLIT):
                shared_high(b)

            def expert_rows(e):
                act.wait_ge(xe_turned, e + 1)
                if e >= 2:
                    act.wait_ge(e_up, e - 1)
                nc.scalar.copy(xdT[:, e % 2].rearrange("p c t -> p (c t)"), y_bank[e % 2][:, 0:D]).then_inc(
                    xe_copied, 1)

            def expert_silu(e):
                act.wait_ge(e_up, e + 1)
                if e >= 2:
                    act.wait_ge(e_h, e - 1)
                nc.scalar.activation(sig[:, e % 2, :], u1_bank[e % 2][:, 0:F], ACT.Silu).then_inc(e_silu, 1)

            def expert_out(e):
                act.wait_ge(e_down, e + 1)
                if e >= 2:
                    act.wait_ge(oe_stored[e % 2], 16 * (e // 2))
                nc.scalar.copy(ye[:, e % 2, :], y_bank[(e + 1) % 2][:, 0:D]).then_inc(e_copied, 1)

            for e in range(E + 1):
                if e < E:
                    expert_rows(e)
                    expert_silu(e)
                if e >= 1:
                    expert_out(e - 1)
            for b in range(SPLIT, B):
                shared_high(b)

        @block.tensor
        def _(pe):
            ident = cst[:, IDENT:IDENT + P]
            pe.wait_ge(ld_cst, 16)
            for b in range(B):
                pe.wait_ge(ld_ctx[chunk_of[b]], 16)
                if b >= 1:
                    pe.wait_ge(v_copied, b)
                for c in range(2):
                    mm = nc.tensor.transpose(X[:, c * P:(c + 1) * P], cs[:, b, c * P:(c + 1) * P], ident)
                mm.then_inc(v_turned, 1)
            pe.wait_ge(cst_copied, 3)
            pe.wait_ge(sones_set, 2)

            def scores(n):
                b, h = divmod(n, H)
                s = b % NSTACK
                if h == 0:
                    pe.wait_ge(ld_st[s], 16 * 5 * ring_pass(b, NSTACK))
                if n >= 3:
                    pe.wait_ge(maxed, n - 2)
                for u in range(2):
                    mm = nc.tensor.matmul(mx_bank[n % 3][:, u * D:(u + 1) * D], qst[0:KA, s, h, u * P:(u + 1) * P],
                                          kst[0:KA, s, h, :], start=True, stop=True)
                mm.then_inc(scored, 1)

            def turn_maxima(b):
                pe.wait_ge(nm_lo, b + 1)
                if b == 0:
                    pe.wait_ge(v_copied, B)
                if b >= 3:
                    pe.wait_ge(x_lo, b - 2)
                nc.tensor.transpose(X[0:48, 0:P // 2].bitcast(BF16),
                                    nm3[:, b % 2].rearrange("p t u -> p (t u)"), identb[:]).then_inc(nm_turned, 1)

            def shifted_scores(n):
                b, h = divmod(n, H)
                s = b % NSTACK
                if h == 0:
                    pe.wait_ge(ld_m[b % 2], 48 * ring_pass(b, 2))
                if n >= 2:
                    pe.wait_ge(exped, n - 1)
                for c in range(2):
                    mm = nc.tensor.matmul(sc_bank[n % 2][:, c * D:(c + 1) * D], kst[0:KT, s, h, c * P:(c + 1) * P],
                                          qst[0:KT, s, h, :], start=True, stop=True)
                mm.then_inc(shifted, 1)

            def weigh_values(g):
                b, u = divmod(g, 2)
                pe.wait_ge(exped, 4 * g + 4)
                if u == 0 and b >= 1:
                    pe.wait_ge(o_lo, b)
                for c in range(2):
                    for j in range(4):
                        mm = nc.tensor.matmul(O[32 * j:32 * j + 32, u * D:(u + 1) * D],
                                              vext[:, b, c, 4 * u + j, :], pt[:, g % 2, j, c * D:(c + 1) * D],
                                              start=(c == 0), stop=(c == 1), skip_group_check=True)
                mm.then_inc(valued, 1)

            def place(b):
                pe.wait_ge(o_lo, b + 1)
                if b >= 1:
                    pe.wait_ge(normed, b)
                for w in range(2):
                    for g in range(2):
                        for k, part in enumerate((ohi, olo)):
                            mm = nc.tensor.matmul(R[:, w * D:(w + 1) * D],
                                                  selr[:, (2 * w + g) * P:(2 * w + g + 1) * P],
                                                  part[:, b % 2, g * D:(g + 1) * D],
                                                  start=(g == 0 and k == 0), stop=(g == 1 and k == 1))
                mm.then_inc(placed, 1)

            def turn_tokens(b):
                pe.wait_ge(x2_made, b + 1)
                pe.wait_ge(nm_row, min(b + 3, B))
                for c in range(DC):
                    mm = nc.tensor.transpose(X[:, c * P:(c + 1) * P], x2[:, b, c * P:(c + 1) * P], ident)
                mm.then_inc(x_turned, 1)

            for s in range(NH + LAG + AFTER):
                if s < NH:
                    scores(s)
                b, rest = divmod(s - H - MROW, H)
                if rest == 0 and 0 <= b < B:
                    turn_maxima(b)
                if 0 <= s - LAG < NH:
                    shifted_scores(s - LAG)
                g, rest = divmod(s - LAG - 3 - VALUE, 4)
                if rest == 0 and 0 <= g < NG:
                    weigh_values(g)
                for offset, work in ((PLACE, place), (TTURN, turn_tokens)):
                    b, rest = divmod(s - LAG - H + 1 - offset, H)
                    if rest == 0 and 0 <= b < B:
                        work(b)

            pe.wait_ge(exped, NH)
            pe.wait_ge(maxed, NH)
            pe.wait_ge(s_lo, 1)

            def w(t, base, width, c, n):
                return t[:, base + c * width:base + c * width + n]

            for b in range(B):
                pe.wait_ge(x_lo, b + 1)
                if b >= 2:
                    pe.wait_ge(h_made, b - 1)
                    pe.wait_ge(lg_copied, b - 1)
                u1, u3 = u1_bank[b % 2][:, 0:F + WG], u3_bank[b % 2][:, 0:F]
                for c in range(DC):
                    for xpart, parts in ((xhi, (shi, slo)), (xlo, (shi,))):
                        for part in parts:
                            a, z = (c == 0 and xpart is xhi and part is shi), (c == DC - 1 and xpart is xlo)
                            nc.tensor.matmul(u1, xpart[:, b, c, :], w(part, S1, F + WG, c, F + WG), start=a, stop=z)
                            mm = nc.tensor.matmul(u3, xpart[:, b, c, :], w(part, S3, F, c, F), start=a, stop=z)
                mm.then_inc(up_done, 1)

            pe.wait_ge(route, ROUTE["oh"])
            pe.wait_ge(h_made, B)
            pe.wait_ge(lg_copied, B)
            pe.wait_ge(ones_set, 2)
            nc.tensor.matmul(u1_bank[0][:, 0:B * E], trib[:], oh[:].rearrange("p b e -> p (b e)"), start=True,
                             stop=False, skip_group_check=True)
            for b in range(B - 1):
                mm = nc.tensor.matmul(u1_bank[0][:, E * (b + 1):B * E].rearrange("p (b e) -> p b e", e=E),
                                      onesb[:], oh[:, b:b + 1, :].broadcast_to([P, B - 1 - b, E]),
                                      start=False, stop=(b == B - 2), skip_group_check=True)
            mm.then_inc(pos_done, 1)

            def turn_hidden(b):
                if b == 0:
                    pe.wait_ge(hpad_set, 1)
                if b >= 2:
                    pe.wait_ge(h_lo, b - 1)
                for c in range(FC):
                    mm = nc.tensor.transpose(ht_bank[b % 2][:, c * P:(c + 1) * P], hs[:, b, c * P:(c + 1) * P], ident)
                mm.then_inc(h_turned, 1)

            def shared_down(b):
                pe.wait_ge(h_lo, b + 1)
                if b >= 2:
                    pe.wait_ge(shared_added, b - 1)
                k = 0
                for c in range(FC):
                    for hpart, part in ((hThi, shi), (hThi, slo), (hTlo, shi)):
                        mm = nc.tensor.matmul(y_bank[b % 2][:, 0:D], hpart[:, c * P:(c + 1) * P],
                                              w(part, S2, D, c, D), start=(k == 0), stop=(k == 3 * FC - 1))
                        k += 1
                mm.then_inc(down_done, 1)

            def shared(first, last):
                turn_hidden(first)
                for b in range(first, last):
                    if b + 1 < last:
                        turn_hidden(b + 1)
                    shared_down(b)

            shared(0, SPLIT)

            def turn_rows(e):
                if e == 0:
                    pe.wait_ge(ld_xe, 16)
                if e < 2:
                    pe.wait_ge(shared_added, SPLIT)
                if e >= 3:
                    pe.wait_ge(e_copied, e - 2)
                for c in range(DC):
                    mm = nc.tensor.transpose(y_bank[e % 2][:, c * P:(c + 1) * P], xe[:, e, c * P:(c + 1) * P], ident)
                mm.then_inc(xe_turned, 1)

            def expert_up(e):
                pe.wait_ge(xe_copied, e + 1)
                pe.wait_ge(ld_w[e % NW], 16 * 4 * ring_pass(e, NW))
                if e == 0:
                    pe.wait_ge(route, ROUTE["cum"])
                if e >= 2:
                    pe.wait_ge(e_h, e - 1)
                for c in range(DC):
                    lhs = xdT[:, e % 2, c, :]
                    nc.tensor.matmul(u1_bank[e % 2][:, 0:F], lhs, w(wraw[:, e % NW], W1, F, c, F),
                                     start=(c == 0), stop=(c == DC - 1))
                    mm = nc.tensor.matmul(u3_bank[e % 2][:, 0:F], lhs, w(wraw[:, e % NW], W3, F, c, F),
                                          start=(c == 0), stop=(c == DC - 1))
                mm.then_inc(e_up, 1)

            def turn_expert_hidden(e):
                pe.wait_ge(e_h, e + 1)
                if e == 0:
                    pe.wait_ge(hpad_set, 2)
                if e >= 2:
                    pe.wait_ge(eh_copied, e - 1)
                else:
                    pe.wait_ge(h_lo, SPLIT)
                for c in range(FC):
                    mm = nc.tensor.transpose(ht_bank[e % 2][:, c * P:(c + 1) * P], he[:, e % 2, c * P:(c + 1) * P],
                                             ident)
                mm.then_inc(eh_turned, 1)

            def expert_down(e):
                pe.wait_ge(eh_copied, e + 1)
                if e + 1 < E:
                    pe.wait_ge(xe_copied, e + 2)
                else:
                    pe.wait_ge(e_copied, e - 1)
                for c in range(FC):
                    rows = P if c < 2 else FL
                    mm = nc.tensor.matmul(y_bank[(e + 1) % 2][:, 0:D], hTe[0:rows, e % 2, c * P:(c + 1) * P],
                                          wraw[0:rows, e % NW, W2 + c * D:W2 + (c + 1) * D],
                                          start=(c == 0), stop=(c == FC - 1))
                mm.then_inc(e_down, 1)

            turn_rows(0)
            for e in range(E + 1):
                if e < E:
                    expert_up(e)
                if e >= 1:
                    turn_expert_hidden(e - 1)
                if e + 1 < E:
                    turn_rows(e + 1)
                if e >= 1:
                    expert_down(e - 1)
            pe.wait_ge(e_copied, E)
            pe.wait_ge(eh_copied, E)
            shared(SPLIT, B)


def kernel(x, ctx_2048, itok_B_779_1933, L0_ffn_Wg, L0_ffn_W1, L0_ffn_W3, L0_ffn_W2, L0_ffn_sw1, L0_ffn_sw3,
           L0_ffn_sw2):
    import concourse.bacc as bacc
    from concourse.bass_utils import run_bass_kernel_spmd

    given = {
        "x": x, "ctx": ctx_2048, "lens": itok_B_779_1933, "wg": L0_ffn_Wg, "w1": L0_ffn_W1, "w3": L0_ffn_W3,
        "w2": L0_ffn_W2, "sw1": L0_ffn_sw1, "sw3": L0_ffn_sw3, "sw2": L0_ffn_sw2, "consts": constants(),
    }
    nc = bacc.Bacc("TRN2", target_bir_lowering=False, num_devices=1)
    arrays, args = {}, []
    for name, a in given.items():
        a = np.ascontiguousarray(a)
        arrays[f"in_{name}"] = a
        args.append(nc.dram_tensor(f"in_{name}", a.shape, mybir.dt.from_np(a.dtype), kind="ExternalInput").ap())
    out = nc.dram_tensor("out", (B, P, D), F32, kind="ExternalOutput").ap()
    block_kernel(nc, *args, out)
    r = run_bass_kernel_spmd(nc, [arrays], core_ids=[0])
    return r.results[0]["out"]
```

```python
from contextlib import ExitStack

import concourse.bass as bass
import numpy as np
from concourse import mybir

F32 = mybir.dt.float32
F32R = mybir.dt.float32r
BF16 = mybir.dt.bfloat16
I32 = mybir.dt.int32
U32 = mybir.dt.uint32
ALU = mybir.AluOpType
ACT = mybir.ActivationFunctionType
AX_X = mybir.AxisListType.X

P = 128
B, D = 8, 256
H, HD = 8, 16
NH = B * H
NG = NH // 4
E, C, F = 8, 128, 352
DC = D // P
FC = 3
FL = F - 2 * P
SCALE = 1.0 / (64 ** 0.5 * float(np.log(20)))
EPS = 1e-5

PART = P * D
QUERY_PARTS = (0, 0, 0, 1, 1, 1, 2)
KEY_PARTS = (0, 1, 2, 0, 1, 2, 0)
SLOTS = len(QUERY_PARTS)
KA = SLOTS * HD
KT = KA + 3
TWO_ONES = float(np.array([0x3F803F80], np.uint32).view(np.float32)[0])
NV = 4
NSTACK = 4
LAG = 15
CHUNKS = ((0, 1), (1, 2), (2, 4), (4, B))

IDENT, TRI, SELV, SELS, ECOL, NUMBER = 0, P, 2 * P, 4 * P, 6 * P, 6 * P + B * E
CONST_COLS = 6 * P + B * E + B

WG = E
S1, S3, S2 = 0, DC * (F + WG), DC * (F + WG) + DC * F
SCOLS = S2 + FC * D
W1, W3, W2 = 0, DC * F, 2 * DC * F
WCOLS = W2 + FC * D
NW = 5
DW = D + 2
NO_TOKEN = 4 * B * P
LOADS = ((0, 1), (1, 4), (4, E))

VALUE, OUT_HI, OUT_LO, PLACE, INV, NORM, STATS, TRSTD, TNORM, TTURN, THI, TLOW = (
    2, 3, 4, 5, 6, 7, 9, 10, 11, 14, 15, 16)
AFTER = 17
VTURN = 7

MROW = 2

X_USERS = sorted([(H * b + VTURN, "values", b) for b in range(B)] + [(H * b + H + MROW, "maxima", b) for b in range(B)]
                 + [(H * b + LAG + H - 1 + TTURN, "tokens", b) for b in range(B)])


ROUTE = {n: i + 1 for i, n in enumerate((
    "lmax", "ldif", "cand", "first", "oh", "lsum", "gate", "cum", "pos", "keep", "slot", "slot2",
    "send", "idx_s"))}


def constants():
    c = np.zeros((P, CONST_COLS), np.float32)
    r = np.arange(P)
    c[r, IDENT + r] = 1.0
    c[:, TRI:TRI + P] = r[:, None] <= r[None, :]
    for g in range(2):
        for j in range(4):
            head = HD * (4 * g + j)
            for d in range(HD):
                c[32 * j + d, SELV + g * P + head + d] = 1.0
                c[32 * j + HD, SELS + g * P + head + d] = 1.0
    c[:, ECOL:NUMBER] = np.tile(E - np.arange(E), B)[None, :]
    c[:, NUMBER:] = P * np.arange(B)[None, :] + r[:, None]
    return c


def block_kernel(nc, x, ctx_in, lens, wg, w1, w3, w2, sw1, sw3, sw2, consts, out):
    with ExitStack() as es:
        def sb(name, shape, dt):
            return es.enter_context(nc.sbuf_tensor(name, shape, dt))

        def sem(name):
            return es.enter_context(nc.semaphore(name))

        q_dram = nc.dram_tensor("q_parts", [B, 3, HD, H, D], BF16, kind="Internal").ap()
        k_dram = nc.dram_tensor("k_parts", [B, 3, HD, H, D], BF16, kind="Internal").ap()
        xd_dram = nc.dram_tensor("expert_rows", [E * C, DW], F32, kind="Internal").ap()
        out_rows = out.rearrange("b p d -> (b p) d")

        cst = sb("cst", [P, CONST_COLS], F32)
        identb = sb("identb", [P, P], BF16)
        trib = sb("trib", [P, P], BF16)
        onesb = sb("onesb", [P, P], BF16)
        selr = sb("selr", [P, 4 * P], F32R)
        xs = sb("xs", [P, B, D], F32)
        cs = sb("cs", [P, B, D], F32)
        qf = sb("qf", [P, B, D], F32)
        rk = sb("rk", [P, B, DW], F32)
        qp = sb("qp", [P, B, 3, D], BF16)
        kp = sb("kp", [P, B, 3, D], BF16)
        qst = sb("qst", [P, NSTACK, H, D], BF16)
        kst = sb("kst", [P, NSTACK, H, D], BF16)
        vext = sb("vext", [P, NV, 2, H, 2 * HD], F32)
        pt = sb("pt", [P, 2, 4, 2 * D], F32)
        st = sb("st", [P, B, 6], F32)
        mv = sb("mv", [P, B, 2], F32)
        lnv = sb("lnv", [P, B], F32)
        rstd = sb("rstd", [P, B], F32)
        rs = sb("rs", [P, B], F32)
        leni = sb("leni", [P, B], I32)
        lenf = sb("lenf", [P, B], F32)
        lnlen = sb("lnlen", [P, B], F32)
        epst = sb("epst", [P, 1], F32)
        nm = sb("nm", [P, 2, H * 2], F32)
        nmr = sb("nmr", [P, 2, H * 2], F32)
        nm3 = sb("nm3", [P, 2, 3, H * 2], BF16)
        mrow = sb("mrow", [3 * H * 2, 2, P], BF16)
        ohi = sb("ohi", [P, 2, 2 * D], F32R)
        olo = sb("olo", [P, 2, 2 * D], F32R)
        lsums = sb("lsums", [P, D], F32)
        rinv = sb("rinv", [P, D], F32)
        units = sb("units", [P, D], F32)
        att0 = sb("att0", [P, D], F32)
        att = sb("att", [P, 2, D], F32)
        st2 = sb("st2", [P, B, 6], F32)
        mv2 = sb("mv2", [P, B, 2], F32)
        lnv2 = sb("lnv2", [P, B], F32)
        rstd2 = sb("rstd2", [P, B], F32)
        x2 = rk
        xhi = sb("xhi", [P, B, DC, P], F32R)
        xlo = sb("xlo", [P, B, DC, P], F32R)
        shi = sb("shi", [P, SCOLS], F32R)
        slo = sb("slo", [P, SCOLS], F32R)
        wraw = sb("wraw", [P, 3, SCOLS], F32)
        pt_flat = pt[:].rearrange("p g j c -> p (g j c)")
        kst_flat = kst[:].rearrange("p n h d -> p (n h d)").bitcast(F32)
        wts = [wraw[:, i, 0:WCOLS] for i in range(3)] + [t[:, 0:WCOLS] for t in (pt_flat, kst_flat)]
        sraw = wraw[:, 0, :]

        sig = cs[:, 0:4, :].rearrange("p b d -> p (b d)")[:, 0:2 * F].rearrange("p (n f) -> p n f", n=2)
        xdT = cs[:, 4:8, :].rearrange("p b (c t) -> p b c t", c=DC)
        hs = qst[:].bitcast(F32).rearrange("p n h d -> p (n h d)")[:, 0:B * FC * P].rearrange(
            "p (b f) -> p b f", b=B)
        he = qf[:, 0:4, :].rearrange("p b d -> p (b d)")[:, 0:2 * FC * P].rearrange("p (n f) -> p n f", n=2)
        hTe = qf[:, 4:8, :].rearrange("p b d -> p (b d)")[:, 0:2 * FC * P].rearrange("p (n f) -> p n f", n=2)
        xe = rk
        hThi = sb("hThi", [P, 2, FC * P], F32R)
        hTlo = sb("hTlo", [P, 2, FC * P], F32R)
        res = qp[:].bitcast(F32).rearrange("p b t d -> p (b t d)")[:, 0:E * D].rearrange(
            "p (e d) -> p e d", e=E)
        zero = sb("zero", [P, DW], F32)
        lg = sb("lg", [P, B, E], F32)
        lmax = sb("lmax", [P, B], F32)
        ldif = sb("ldif", [P, B, E], F32)
        lexp = sb("lexp", [P, B, E], F32)
        lsum = sb("lsum", [P, B], F32)
        gate = sb("gate", [P, B], F32)
        cand = sb("cand", [P, B, E], F32)
        first = sb("first", [P, B], F32)
        oh = sb("oh", [P, B, E], BF16)
        cum = sb("cum", [P, B, E], F32)
        pos = sb("pos", [P, B], F32)
        keep = sb("keep", [P, B], F32)
        slot = sb("slot", [P, B], F32)
        slot2 = sb("slot2", [P, B], F32)
        send = sb("send", [P, B], F32)
        idx_s = sb("idx_s", [P, B], U32)

        bank = [es.enter_context(nc.psum_tensor(f"bank{i}", [P, 512], F32)) for i in range(8)]
        mx_bank, sc_bank, O, R, X = bank[0:3], bank[3:5], bank[5], bank[6], bank[7]
        u1_bank, u3_bank, ht_bank, y_bank = bank[0:2], bank[2:4], bank[4:6], bank[6:8]

        ld_cst, ld_len = sem("ld_cst"), sem("ld_len")
        ld_ctx = [sem(f"ld_ctx{i}") for i in range(len(CHUNKS))]
        ld_x = [sem(f"ld_x{i}") for i in range(len(CHUNKS))]
        ld_shared = sem("ld_shared")
        ld_w = [sem(f"ld_w{i}") for i in range(NW)]
        st_q = [sem(f"st_q{i}") for i in range(len(CHUNKS))]
        st_k = [sem(f"st_k{i}") for i in range(len(CHUNKS))]
        ld_st = [sem(f"ld_st{i}") for i in range(NSTACK)]
        ld_m = [sem(f"ld_m{i}") for i in range(2)]
        xd_zeroed, xd_sent = sem("xd_zeroed"), sem("xd_sent")
        ld_xe = [sem(f"ld_xe{i}") for i in range(len(LOADS))]
        base_stored, gathered, out_sent = sem("base_stored"), sem("gathered"), sem("out_sent")
        empty_set, numbered = sem("empty_set"), sem("numbered")
        eps_set, ones_set, sones_set, pad_set, hpad_set = (
            sem(s) for s in ("eps_set", "ones_set", "sones_set", "pad_set", "hpad_set"))
        cst_copied, len_f, len_ln = sem("cst_copied"), sem("len_f"), sem("len_ln")
        k_hi, k_rest, k_mid, k_lo = (sem(s) for s in ("k_hi", "k_rest", "k_mid", "k_lo"))
        q_hi, q_rest, q_mid, q_lo = (sem(s) for s in ("q_hi", "q_rest", "q_mid", "q_lo"))
        q_stats, q_mv, q_ln, q_rstd, q_rs, q_made = (
            sem(s) for s in ("q_stats", "q_mv", "q_ln", "q_rstd", "q_rs", "q_made"))
        v_turned, v_copied = sem("v_turned"), sem("v_copied")
        scored, maxed, nm_hi, nm_rest, nm_mid, nm_lo = (
            sem(s) for s in ("scored", "maxed", "nm_hi", "nm_rest", "nm_mid", "nm_lo"))
        nm_turned, nm_row = sem("nm_turned"), sem("nm_row")
        shifted, exped, valued = sem("shifted"), sem("exped"), sem("valued")
        o_hi, o_lo, placed, sum_ln, inverted, unit, rough, normed, added = (
            sem(s) for s in ("o_hi", "o_lo", "placed", "sum_ln", "inverted", "unit", "rough", "normed", "added"))
        x_stats, x_mv, x_ln, x_rstd, x2_made = (sem(s) for s in ("x_stats", "x_mv", "x_ln", "x_rstd", "x2_made"))
        x_turned, x_hi, x_lo = sem("x_turned"), sem("x_hi"), sem("x_lo")
        s_hi, s_lo = sem("s_hi"), sem("s_lo")
        up_done, silu_done, lg_copied, h_made = (sem(s) for s in ("up_done", "silu_done", "lg_copied", "h_made"))
        route, route_exp, pos_done = sem("route"), sem("route_exp"), sem("pos_done")
        h_turned, h_hi, h_lo, down_done, shared_added = (
            sem(s) for s in ("h_turned", "h_hi", "h_lo", "down_done", "shared_added"))
        xe_turned, xe_copied, eh_turned, eh_copied, e_up, e_silu, e_h, e_down, e_out = (
            sem(s) for s in ("xe_turned", "xe_copied", "eh_turned", "eh_copied", "e_up", "e_silu", "e_h",
                             "e_down", "e_out"))

        block = es.enter_context(nc.Block())

        def ring_pass(n, size):
            return n // size + 1

        chunk_of = [next(i for i, (a, z) in enumerate(CHUNKS) if a <= b < z) for b in range(B)]

        @block.sync
        def _(sp):
            for i, (a, z) in enumerate(CHUNKS):
                sp.dma_start(cs[:, a:z, :], ctx_in[a:z].rearrange("b p d -> p b d")).then_inc(ld_ctx[i], 16)
                sp.dma_start(xs[:, a:z, :], x[a:z].rearrange("b p d -> p b d")).then_inc(ld_x[i], 16)
                if i == 0:
                    sp.dma_start(leni[:], bass.AP(tensor=lens.tensor, offset=lens.offset,
                                                  ap=[[0, P], [1, B]])).then_inc(ld_len, 16)
                    sp.dma_start(cst[:], consts).then_inc(ld_cst, 16)

            def store(parts, dram, done, ready, i):
                a, z = CHUNKS[i]
                if z - a == 1:
                    for part in range(3):
                        sp.wait_ge(ready[part], i + 1)
                        sp.dma_start(
                            bass.AP(tensor=dram.tensor, offset=(a * 3 + part) * PART,
                                    ap=[[D, H], [H * D, HD], [1, D]]),
                            parts[:, a, part, :]).then_inc(done[i], 16)
                else:
                    sp.wait_ge(ready[2], i + 1)
                    for h in range(H):
                        sp.dma_start(
                            bass.AP(tensor=dram.tensor, offset=a * 3 * PART + h * D,
                                    ap=[[H * D, HD], [PART, 3 * (z - a)], [1, D]]),
                            parts[HD * h:HD * h + HD, a:z, :, :].rearrange("p b t d -> p (b t) d")
                        ).then_inc(done[i], 16)

            def load_stack(b):
                s, i = b % NSTACK, chunk_of[b]
                n = 3 if i < 2 else H
                if b >= NSTACK:
                    sp.wait_ge(shifted, H * (b - NSTACK + 1))
                sp.wait_ge(sones_set, 1 if b == 0 else 2)
                sp.wait_ge(st_k[i], 16 * n)
                base = b * 3 * PART
                row = H * D
                kd, qd = kst[:, s].rearrange("p h d -> p (h d)"), qst[:, s].rearrange("p h d -> p (h d)")
                sp.dma_start(kd[0:96, :], bass.AP(tensor=k_dram.tensor, offset=base,
                                                  ap=[[0, 2], [row, 48], [1, row]])).then_inc(ld_st[s], 16)
                sp.dma_start(kd[96:112, :], bass.AP(tensor=k_dram.tensor, offset=base,
                                                    ap=[[row, HD], [1, row]])).then_inc(ld_st[s], 16)
                sp.wait_ge(st_q[i], 16 * n)
                for part in range(2):
                    sp.dma_start(qd[48 * part:48 * part + 48, :],
                                 bass.AP(tensor=q_dram.tensor, offset=base + part * PART,
                                         ap=[[0, 3], [row, HD], [1, row]])).then_inc(ld_st[s], 16)
                sp.dma_start(qd[96:112, :], bass.AP(tensor=q_dram.tensor, offset=base + 2 * PART,
                                                    ap=[[row, HD], [1, row]])).then_inc(ld_st[s], 16)

            def load_maxima(b):
                sp.wait_ge(nm_row, b + 1)
                for t in range(3):
                    sp.dma_start(qst[KA + t:KA + t + 1, b % NSTACK].rearrange("p h (u c) -> p (h u) c", u=2),
                                 mrow[16 * t:16 * t + 16, b % 2, :]).then_inc(ld_m[b % 2], 16)

            def load_expert(e):
                n = e % NW
                if e == 0:
                    sp.wait_ge(s_lo, 1)
                if e == 3:
                    sp.wait_ge(valued, NG)
                if e == 4:
                    sp.wait_ge(shifted, NH)
                if e >= NW:
                    sp.wait_ge(e_down, e - NW + 1)
                t = wts[n]
                sp.dma_start(t[:, W1:W3].rearrange("p (c f) -> p c f", c=DC),
                             w1[e].rearrange("(c p) f -> p c f", p=P)).then_inc(ld_w[n], 16)
                sp.dma_start(t[:, W3:W2].rearrange("p (c f) -> p c f", c=DC),
                             w3[e].rearrange("(c p) f -> p c f", p=P)).then_inc(ld_w[n], 16)
                sp.dma_start(t[:, W2:W2 + 2 * D].rearrange("p (c d) -> p c d", c=2),
                             w2[e, 0:2 * P].rearrange("(c p) d -> p c d", p=P)).then_inc(ld_w[n], 16)
                sp.dma_start(t[0:FL, W2 + 2 * D:WCOLS], w2[e, 2 * P:F]).then_inc(ld_w[n], 16)

            kr, qr = (k_hi, k_mid, k_lo), (q_hi, q_mid, q_lo)
            for i in range(2):
                store(kp, k_dram, st_k, kr, i)
                store(qp, q_dram, st_q, qr, i)
                load_stack(i)
            store(kp, k_dram, st_k, kr, 2)
            store(qp, q_dram, st_q, qr, 2)
            load_stack(2)
            load_stack(3)
            load_maxima(0)
            store(kp, k_dram, st_k, kr, 3)
            store(qp, q_dram, st_q, qr, 3)
            load_maxima(1)
            s1 = sraw[:, S1:S3].rearrange("p (c f) -> p c f", c=DC)
            sp.dma_start(s1[:, :, 0:F], sw1.rearrange("(c p) f -> p c f", p=P)).then_inc(ld_shared, 16)
            sp.dma_start(s1[:, :, F:], wg.rearrange("(c p) f -> p c f", p=P)).then_inc(ld_shared, 16)
            sp.dma_start(sraw[:, S3:S2].rearrange("p (c f) -> p c f", c=DC),
                         sw3.rearrange("(c p) f -> p c f", p=P)).then_inc(ld_shared, 16)
            sp.dma_start(sraw[:, S2:S2 + 2 * D].rearrange("p (c d) -> p c d", c=2),
                         sw2[0:2 * P].rearrange("(c p) d -> p c d", p=P)).then_inc(ld_shared, 16)
            sp.wait_ge(pad_set, 1)
            sp.dma_start(sraw[0:FL, S2 + 2 * D:], sw2[2 * P:F]).then_inc(ld_shared, 16)
            for b in range(NSTACK, B):
                load_stack(b)
                load_maxima(b - 2)
            load_maxima(B - 2)
            load_maxima(B - 1)
            sp.wait_ge(empty_set, 2)
            sp.dma_start(xd_dram.rearrange("(n p) d -> p n d", p=P),
                         zero[:].unsqueeze(1).broadcast_to([P, E, DW])).then_inc(xd_zeroed, 16)
            for e in range(NW):
                load_expert(e)
            sp.wait_ge(xd_sent, 16 * B)
            xd = xd_dram.rearrange("(n p) d -> p n d", p=P)
            for i, (a, z) in enumerate(LOADS):
                sp.dma_start(xe[:, a:z, :], xd[:, a:z, :]).then_inc(ld_xe[i], 16)
            for a, z in ((0, B // 2), (B // 2, B)):
                sp.wait_ge(shared_added, z)
                sp.dma_start(out[a:z].rearrange("b p d -> p b d"), xs[:, a:z, :]).then_inc(base_stored, 16)
            for e in range(NW, E):
                load_expert(e)

        @block.gpsimd
        def _(pool):
            def ones_rows(first, last):
                n = kst[96:P, first:last].rearrange("p n h d -> p (n h d)").bitcast(F32)
                nc.gpsimd.memset(n, TWO_ONES).then_inc(sones_set, 1)

            nc.gpsimd.memset(epst[:], EPS).then_inc(eps_set, 1)
            pool.wait_ge(eps_set, 1)
            ones_rows(0, 1)
            pool.wait_ge(sones_set, 1)
            for i, (a, z) in enumerate(CHUNKS):
                pool.wait_ge(k_hi, i + 1)
                nc.gpsimd.tensor_tensor(rk[:, a:z, 0:D], cs[:, a:z, :], kp[:, a:z, 0, :],
                                        ALU.subtract).then_inc(k_rest, 1)
                pool.wait_ge(k_mid, i + 1)
                nc.gpsimd.tensor_tensor(kp[:, a:z, 2, :], rk[:, a:z, 0:D], kp[:, a:z, 1, :],
                                        ALU.subtract).then_inc(k_lo, 1)
                if i == 0:
                    pool.wait_ge(k_lo, 1)
                    ones_rows(1, NSTACK)
                    pool.wait_ge(sones_set, 2)
                if i == 1:
                    nc.gpsimd.memset(vext[:, :, :, :, HD:], 1.0).then_inc(ones_set, 1)
                    nc.gpsimd.memset(onesb[:], 1.0).then_inc(ones_set, 1)
                    pool.wait_ge(ones_set, 2)
                    nc.gpsimd.memset(sraw[FL:P, S2 + 2 * D:], 0.0).then_inc(pad_set, 1)
                    pool.wait_ge(pad_set, 1)
            nc.gpsimd.memset(zero[:], 0.0).then_inc(empty_set, 1)
            pool.wait_ge(empty_set, 1)
            nc.gpsimd.memset(zero[:, D:D + 1].bitcast(U32), NO_TOKEN).then_inc(empty_set, 1)

            def split_maxima(b):
                n = b % 2
                pool.wait_ge(maxed, H * (b + 1))
                if b >= 2:
                    pool.wait_ge(nm_turned, b - 1)
                nc.gpsimd.tensor_copy(nm3[:, n, 0, :], nm[:, n, :]).then_inc(nm_hi, 1)
                pool.wait_ge(nm_hi, b + 1)
                nc.gpsimd.tensor_tensor(nmr[:, n, :], nm[:, n, :], nm3[:, n, 0, :], ALU.subtract).then_inc(nm_rest, 1)
                pool.wait_ge(nm_rest, b + 1)
                nc.gpsimd.tensor_copy(nm3[:, n, 1, :], nmr[:, n, :]).then_inc(nm_mid, 1)
                pool.wait_ge(nm_mid, b + 1)
                nc.gpsimd.tensor_tensor(nm3[:, n, 2, :], nmr[:, n, :], nm3[:, n, 1, :], ALU.subtract).then_inc(nm_lo, 1)

            def add_attention(b):
                pool.wait_ge(normed, b + 1)
                nc.gpsimd.tensor_tensor(xs[:, b, :], xs[:, b, :], att[:, b % 2, :], ALU.subtract).then_inc(added, 1)

            for b in range(B):
                if b >= 3:
                    add_attention(b - 3)
                split_maxima(b)
                if b == 3:
                    pool.wait_ge(s_hi, 1)
                    nc.gpsimd.tensor_tensor(slo[:], sraw, shi[:].bitcast(F32), ALU.subtract).then_inc(s_lo, 1)
            for b in range(B - 3, B):
                add_attention(b)

            pool.wait_ge(xd_zeroed, 16)
            pool.wait_ge(x2_made, B)
            pool.wait_ge(route, ROUTE["idx_s"])
            pool.wait_ge(numbered, 2)
            for b in range(B):
                nc.gpsimd.indirect_dma_start(
                    xd_dram, bass.IndirectOffsetOnAxis(ap=idx_s[:, b:b + 1], axis=0), x2[:, b, :], None,
                    bounds_check=E * C - 1, oob_is_err=False).then_inc(xd_sent, 16)

            def number(e):
                return bass.IndirectOffsetOnAxis(ap=xe[:, e, D:D + 1].bitcast(U32), axis=0)

            for i, (a, z) in enumerate(CHUNKS):
                pool.wait_ge(st_q[i], 16 * (3 if z - a == 1 else H))
            pool.wait_ge(base_stored, 32)
            for i, (a, z) in enumerate(LOADS):
                pool.wait_ge(ld_xe[i], 16)
                for e in range(a, z):
                    nc.gpsimd.indirect_dma_start(
                        res[:, e, :], None, out_rows, number(e),
                        bounds_check=B * P - 1, oob_is_err=False).then_inc(gathered, 16)
            pool.wait_ge(gathered, 16 * E)
            for e in range(E):
                pool.wait_ge(e_out, e + 1)
                nc.gpsimd.indirect_dma_start(
                    out_rows, number(e), res[:, e, :], None,
                    bounds_check=B * P - 1, oob_is_err=False).then_inc(out_sent, 16)
            pool.wait_ge(out_sent, 16 * E)

        @block.vector
        def _(dve):
            dve.wait_ge(ld_cst, 16)
            nc.vector.tensor_copy(identb[:], cst[:, IDENT:IDENT + P]).then_inc(cst_copied, 1)
            nc.vector.tensor_copy(trib[:], cst[:, TRI:TRI + P]).then_inc(cst_copied, 1)
            nc.vector.tensor_copy(selr[:], cst[:, SELV:SELV + 4 * P]).then_inc(cst_copied, 1)
            dve.wait_ge(ld_len, 16)
            nc.vector.tensor_copy(lenf[:], leni[:]).then_inc(len_f, 1)

            def queries(i):
                a, z = CHUNKS[i]
                dve.wait_ge(ld_x[i], 16)
                for b in range(a, z):
                    nc.vector.bn_stats(st[:, b, :], xs[:, b, :]).then_inc(q_stats, 1)
                for b in range(a, z):
                    dve.wait_ge(q_stats, b + 1)
                    nc.vector.bn_aggr(mv[:, b, :], st[:, b, :]).then_inc(q_mv, 1)
                dve.wait_ge(q_rstd, i + 1)
                dve.wait_ge(len_ln, 1)
                nc.vector.scalar_tensor_tensor(rs[:, a:z], rstd[:, a:z], SCALE, lnlen[:, a:z],
                                               ALU.mult, ALU.mult).then_inc(q_rs, 1)
                dve.wait_ge(q_rs, i + 1)
                for b in range(a, z):
                    nc.vector.tensor_scalar(qf[:, b, :], xs[:, b, :], mv[:, b, 0:1], rs[:, b:b + 1],
                                            ALU.subtract, ALU.mult).then_inc(q_made, 1)

            def split_queries(i):
                a, z = CHUNKS[i]
                dve.wait_ge(q_hi, i + 1)
                nc.vector.tensor_tensor(qf[:, a:z, :], qf[:, a:z, :], qp[:, a:z, 0, :],
                                        ALU.subtract).then_inc(q_rest, 1)
                dve.wait_ge(q_mid, i + 1)
                nc.vector.tensor_tensor(qp[:, a:z, 2, :], qf[:, a:z, :], qp[:, a:z, 1, :],
                                        ALU.subtract).then_inc(q_lo, 1)

            for i in range(len(CHUNKS)):
                queries(i)
                split_queries(i)

            def maximum(n):
                b, h = divmod(n, H)
                dve.wait_ge(scored, n + 1)
                if h == 0 and b >= 2:
                    dve.wait_ge(nm_lo, b - 1)
                nc.vector.tensor_reduce(nm[:, b % 2, 2 * h:2 * h + 2],
                                        mx_bank[n % 3][:].rearrange("p (u c) -> p u c", u=2),
                                        AX_X, ALU.max, negate=True).then_inc(maxed, 1)

            def low_output(b):
                dve.wait_ge(o_hi, b + 1)
                nc.vector.tensor_tensor(olo[:, b % 2, :], O[:], ohi[:, b % 2, :].bitcast(F32),
                                        ALU.subtract).then_inc(o_lo, 1)

            def normalise(b):
                dve.wait_ge(inverted, b + 1)
                nc.vector.tensor_tensor(units[:], R[:, D:], rinv[:], ALU.mult).then_inc(unit, 1)
                nc.vector.tensor_tensor(att0[:], R[:, 0:D], rinv[:], ALU.mult).then_inc(rough, 1)
                dve.wait_ge(unit, b + 1)
                dve.wait_ge(rough, b + 1)
                if b >= 2:
                    dve.wait_ge(added, b - 1)
                nc.vector.scalar_tensor_tensor(att[:, b % 2, :], units[:], 2.0, att0[:], ALU.subtract,
                                               ALU.mult).then_inc(normed, 1)

            def token_stats(b):
                dve.wait_ge(added, b + 1)
                nc.vector.bn_stats(st2[:, b, :], xs[:, b, :]).then_inc(x_stats, 1)
                dve.wait_ge(x_stats, b + 1)
                nc.vector.bn_aggr(mv2[:, b, :], st2[:, b, :]).then_inc(x_mv, 1)

            def token_norm(b):
                dve.wait_ge(x_rstd, b + 1)
                nc.vector.tensor_scalar(x2[:, b, 0:D], xs[:, b, :], mv2[:, b, 0:1], rstd2[:, b:b + 1],
                                        ALU.subtract, ALU.mult).then_inc(x2_made, 1)

            def low_tokens(b):
                dve.wait_ge(x_hi, b + 1)
                nc.vector.tensor_tensor(xlo[:, b].rearrange("p c t -> p (c t)"), X[:, 0:D],
                                        xhi[:, b].rearrange("p c t -> p (c t)").bitcast(F32),
                                        ALU.subtract).then_inc(x_lo, 1)

            for s in range(NH + LAG + AFTER):
                if s < NH:
                    maximum(s)
                for offset, work in ((OUT_LO, low_output), (NORM, normalise), (STATS, token_stats),
                                     (TNORM, token_norm), (TLOW, low_tokens)):
                    b, rest = divmod(s - LAG - H + 1 - offset, H)
                    if rest == 0 and 0 <= b < B:
                        work(b)

            dve.wait_ge(shifted, NH)
            nc.vector.memset(hs[:, :, F:], 0.0).then_inc(hpad_set, 1)
            for b in range(B):
                dve.wait_ge(silu_done, b + 1)
                nc.vector.tensor_tensor(hs[:, b, 0:F], u3_bank[b % 2][:, 0:F], sig[:, b % 2, :],
                                        ALU.mult).then_inc(h_made, 1)

            nc.vector.tensor_copy(x2[:, :, D:D + 1].bitcast(U32), cst[:, NUMBER:].unsqueeze(2)).then_inc(numbered, 1)

            def bc(t):
                return t[:].unsqueeze(2).broadcast_to([P, B, E])

            dve.wait_ge(lg_copied, B)
            nc.vector.tensor_reduce(lmax[:], lg[:], AX_X, ALU.max).then_inc(route, 1)
            dve.wait_ge(route, ROUTE["lmax"])
            nc.vector.tensor_tensor(ldif[:], lg[:], bc(lmax), ALU.subtract).then_inc(route, 1)
            dve.wait_ge(route, ROUTE["ldif"])
            nc.vector.scalar_tensor_tensor(
                cand[:].rearrange("p b e -> p (b e)"), ldif[:].rearrange("p b e -> p (b e)"), 0.0,
                cst[:, ECOL:ECOL + B * E], ALU.is_ge, ALU.mult).then_inc(route, 1)
            dve.wait_ge(route, ROUTE["cand"])
            nc.vector.tensor_reduce(first[:], cand[:], AX_X, ALU.max).then_inc(route, 1)
            dve.wait_ge(route, ROUTE["first"])
            nc.vector.tensor_tensor(oh[:], cand[:], bc(first), ALU.is_equal).then_inc(route, 1)
            dve.wait_ge(route_exp, 1)
            nc.vector.tensor_reduce(lsum[:], lexp[:], AX_X, ALU.add).then_inc(route, 1)
            dve.wait_ge(route, ROUTE["lsum"])
            nc.vector.reciprocal(gate[:], lsum[:]).then_inc(route, 1)
            dve.wait_ge(route, ROUTE["gate"])
            nc.vector.tensor_copy(x2[:, :, D + 1:DW], gate[:].unsqueeze(2)).then_inc(numbered, 1)
            dve.wait_ge(pos_done, 1)
            nc.vector.tensor_tensor(cum[:], u1_bank[0][:, 0:B * E].rearrange("p (b e) -> p b e", b=B),
                                    oh[:], ALU.mult).then_inc(route, 1)
            dve.wait_ge(route, ROUTE["cum"])
            nc.vector.tensor_reduce(pos[:], cum[:], AX_X, ALU.add).then_inc(route, 1)
            dve.wait_ge(route, ROUTE["pos"])
            nc.vector.tensor_scalar(keep[:], pos[:], float(C), None, ALU.is_le).then_inc(route, 1)
            nc.vector.scalar_tensor_tensor(slot[:], first[:], -float(C), pos[:], ALU.mult,
                                           ALU.add).then_inc(route, 1)
            dve.wait_ge(route, ROUTE["slot"])
            nc.vector.tensor_scalar(slot2[:], slot[:], float(E * C - 1), None, ALU.add).then_inc(route, 1)
            dve.wait_ge(route, ROUTE["slot2"])
            nc.vector.scalar_tensor_tensor(send[:], keep[:], -float(2 * E * C), slot2[:], ALU.mult,
                                           ALU.add).then_inc(route, 1)
            dve.wait_ge(route, ROUTE["send"])
            nc.vector.tensor_scalar(idx_s[:], send[:], float(2 * E * C), None, ALU.add).then_inc(route, 1)

            def shared_low(b):
                dve.wait_ge(h_hi, b + 1)
                nc.vector.tensor_tensor(hTlo[:, b % 2], ht_bank[b % 2][:, 0:FC * P], hThi[:, b % 2].bitcast(F32),
                                        ALU.subtract).then_inc(h_lo, 1)

            def shared_add(b):
                dve.wait_ge(down_done, b + 1)
                nc.vector.tensor_tensor(xs[:, b, :], y_bank[b % 2][:, 0:D], xs[:, b, :],
                                        ALU.add).then_inc(shared_added, 1)

            def expert_hidden(e):
                dve.wait_ge(e_silu, e + 1)
                if e >= 2:
                    dve.wait_ge(eh_turned, e - 1)
                nc.vector.tensor_tensor(he[:, e % 2, 0:F], u3_bank[e % 2][:, 0:F], sig[:, e % 2, :],
                                        ALU.mult).then_inc(e_h, 1)

            def expert_hT(e):
                dve.wait_ge(eh_turned, e + 1)
                if e >= 2:
                    dve.wait_ge(e_down, e - 1)
                nc.vector.tensor_copy(hTe[:, e % 2, :], ht_bank[e % 2][:, 0:FC * P]).then_inc(eh_copied, 1)

            def expert_out(e):
                dve.wait_ge(gathered, 16 * E)
                dve.wait_ge(e_down, e + 1)
                nc.vector.scalar_tensor_tensor(res[:, e, :], y_bank[e % 2][:, 0:D], xe[:, e, D + 1:DW], res[:, e, :],
                                               ALU.mult, ALU.add).then_inc(e_out, 1)

            shared_low(0)
            for b in range(B):
                if b + 1 < B:
                    shared_low(b + 1)
                shared_add(b)
            dve.wait_ge(q_lo, len(CHUNKS))
            nc.vector.memset(he[:, :, F:], 0.0).then_inc(hpad_set, 1)
            for e in range(E + 2):
                if 1 <= e <= E:
                    expert_hT(e - 1)
                if e < E:
                    expert_hidden(e)
                if e >= 2:
                    expert_out(e - 2)

        @block.scalar
        def _(act):
            nc.scalar.preload_act_table_set("natural_log_exp_and_others")
            act.wait_ge(eps_set, 1)

            def split_keys(i):
                a, z = CHUNKS[i]
                act.wait_ge(ld_ctx[i], 16)
                nc.scalar.copy(kp[:, a:z, 0, :], cs[:, a:z, :]).then_inc(k_hi, 1)

            def mid_keys(i):
                a, z = CHUNKS[i]
                act.wait_ge(k_rest, i + 1)
                nc.scalar.copy(kp[:, a:z, 1, :], rk[:, a:z, 0:D]).then_inc(k_mid, 1)

            def query_rstd(i):
                a, z = CHUNKS[i]
                act.wait_ge(q_mv, z)
                nc.scalar.activation(lnv[:, a:z], mv[:, a:z, 1], ACT.Ln, bias=epst[:, 0:1]).then_inc(q_ln, 1)
                act.wait_ge(q_ln, i + 1)
                nc.scalar.activation(rstd[:, a:z], lnv[:, a:z], ACT.Exp, scale=-0.5).then_inc(q_rstd, 1)

            def split_q(i):
                a, z = CHUNKS[i]
                act.wait_ge(q_made, z)
                nc.scalar.copy(qp[:, a:z, 0, :], qf[:, a:z, :]).then_inc(q_hi, 1)
                act.wait_ge(q_rest, i + 1)
                nc.scalar.copy(qp[:, a:z, 1, :], qf[:, a:z, :]).then_inc(q_mid, 1)

            def values(b):
                act.wait_ge(v_turned, b + 1)
                if b == 0:
                    act.wait_ge(ones_set, 1)
                if b >= NV:
                    act.wait_ge(valued, 2 * (b - NV) + 2)
                nc.scalar.copy(vext[:, b % NV, :, :, 0:HD],
                               X[:, 0:2 * P].rearrange("p (c h d) -> p c h d", c=2, h=H)).then_inc(v_copied, 1)

            split_keys(0)
            act.wait_ge(len_f, 1)
            nc.scalar.activation(lnlen[:], lenf[:], ACT.Ln).then_inc(len_ln, 1)
            query_rstd(0)
            mid_keys(0)
            split_q(0)
            for i in range(1, len(CHUNKS)):
                split_keys(i)
                query_rstd(i)
                mid_keys(i)
                split_q(i)
            def maxima_rows(b):
                act.wait_ge(nm_turned, b + 1)
                if b >= 2:
                    act.wait_ge(ld_m[b % 2], 48 * (b // 2))
                nc.scalar.copy(mrow[:, b % 2, :], X[0:48, 0:P // 2].bitcast(BF16)).then_inc(nm_row, 1)

            def exponentials(n):
                g = n // 4
                act.wait_ge(shifted, n + 1)
                if g >= 2:
                    act.wait_ge(valued, g - 1)
                nc.scalar.activation(pt[:, g % 2, n % 4, :], sc_bank[n % 2][:], ACT.Exp).then_inc(exped, 1)

            def high_output(b):
                act.wait_ge(valued, 2 * b + 2)
                if b >= 2:
                    act.wait_ge(placed, b - 1)
                nc.scalar.copy(ohi[:, b % 2, :], O[:]).then_inc(o_hi, 1)

            def invert_sums(b):
                act.wait_ge(placed, b + 1)
                nc.scalar.activation(lsums[:], R[:, D:], ACT.Ln).then_inc(sum_ln, 1)
                act.wait_ge(sum_ln, b + 1)
                if b >= 1:
                    act.wait_ge(normed, b)
                nc.scalar.activation(rinv[:], lsums[:], ACT.Exp, scale=-1.0).then_inc(inverted, 1)

            def token_rstd(b):
                act.wait_ge(x_mv, b + 1)
                nc.scalar.activation(lnv2[:, b:b + 1], mv2[:, b, 1:2], ACT.Ln, bias=epst[:, 0:1]).then_inc(x_ln, 1)
                act.wait_ge(x_ln, b + 1)
                nc.scalar.activation(rstd2[:, b:b + 1], lnv2[:, b:b + 1], ACT.Exp, scale=-0.5).then_inc(x_rstd, 1)

            def high_tokens(b):
                act.wait_ge(x_turned, b + 1)
                nc.scalar.copy(xhi[:, b].rearrange("p c t -> p (c t)"), X[:, 0:D]).then_inc(x_hi, 1)

            for s in range(NH + LAG + AFTER):
                b, rest = divmod(s - H - MROW, H)
                if rest == 0 and 0 <= b < B:
                    maxima_rows(b)
                b, rest = divmod(s - VTURN, H)
                if rest == 0 and 0 <= b < B:
                    values(b)
                if 0 <= s - LAG < NH:
                    exponentials(s - LAG)
                for offset, work in ((OUT_HI, high_output), (INV, invert_sums), (TRSTD, token_rstd), (THI, high_tokens)):
                    b, rest = divmod(s - LAG - H + 1 - offset, H)
                    if rest == 0 and 0 <= b < B:
                        work(b)
                if s == 20:
                    act.wait_ge(ld_shared, 16 * 5)
                    nc.scalar.copy(shi[:], sraw).then_inc(s_hi, 1)

            for b in range(B):
                act.wait_ge(up_done, b + 1)
                if b >= 2:
                    act.wait_ge(h_made, b - 1)
                nc.scalar.activation(sig[:, b % 2, :], u1_bank[b % 2][:, 0:F], ACT.Silu).then_inc(silu_done, 1)
                nc.scalar.copy(lg[:, b, :], u1_bank[b % 2][:, F:F + E]).then_inc(lg_copied, 1)
            act.wait_ge(route, ROUTE["ldif"])
            nc.scalar.activation(lexp[:], ldif[:], ACT.Exp).then_inc(route_exp, 1)

            def shared_high(b):
                act.wait_ge(h_turned, b + 1)
                if b >= 2:
                    act.wait_ge(down_done, b - 1)
                nc.scalar.copy(hThi[:, b % 2], ht_bank[b % 2][:, 0:FC * P]).then_inc(h_hi, 1)

            for b in range(B):
                shared_high(b)

            def expert_rows(e):
                act.wait_ge(xe_turned, e + 1)
                if e >= 2:
                    act.wait_ge(e_up, e - 1)
                nc.scalar.copy(xdT[:, e % 2].rearrange("p c t -> p (c t)"), y_bank[e % 2][:, 0:D]).then_inc(
                    xe_copied, 1)

            def expert_silu(e):
                act.wait_ge(e_up, e + 1)
                if e >= 2:
                    act.wait_ge(e_h, e - 1)
                nc.scalar.activation(sig[:, e % 2, :], u1_bank[e % 2][:, 0:F], ACT.Silu).then_inc(e_silu, 1)

            expert_rows(0)
            for e in range(E):
                expert_silu(e)
                if e + 1 < E:
                    expert_rows(e + 1)

        @block.tensor
        def _(pe):
            ident = cst[:, IDENT:IDENT + P]
            pe.wait_ge(ld_cst, 16)

            def x_free(kind, b):
                n = next(i for i, u in enumerate(X_USERS) if u[1:] == (kind, b))
                if n:
                    _, last, k = X_USERS[n - 1]
                    pe.wait_ge({"values": v_copied, "maxima": nm_row, "tokens": x_lo}[last], k + 1)

            def turn_values(b):
                pe.wait_ge(ld_ctx[chunk_of[b]], 16)
                x_free("values", b)
                for c in range(2):
                    mm = nc.tensor.transpose(X[:, c * P:(c + 1) * P], cs[:, b, c * P:(c + 1) * P], ident)
                mm.then_inc(v_turned, 1)

            pe.wait_ge(cst_copied, 3)
            pe.wait_ge(sones_set, 2)

            def scores(n):
                b, h = divmod(n, H)
                s = b % NSTACK
                if h == 0:
                    pe.wait_ge(ld_st[s], 16 * 5 * ring_pass(b, NSTACK))
                if n >= 3:
                    pe.wait_ge(maxed, n - 2)
                for u in range(2):
                    mm = nc.tensor.matmul(mx_bank[n % 3][:, u * D:(u + 1) * D], qst[0:KA, s, h, u * P:(u + 1) * P],
                                          kst[0:KA, s, h, :], start=True, stop=True)
                mm.then_inc(scored, 1)

            def turn_maxima(b):
                pe.wait_ge(nm_lo, b + 1)
                x_free("maxima", b)
                nc.tensor.transpose(X[0:48, 0:P // 2].bitcast(BF16),
                                    nm3[:, b % 2].rearrange("p t u -> p (t u)"), identb[:]).then_inc(nm_turned, 1)

            def shifted_scores(n):
                b, h = divmod(n, H)
                s = b % NSTACK
                if h == 0:
                    pe.wait_ge(ld_m[b % 2], 48 * ring_pass(b, 2))
                if n >= 2:
                    pe.wait_ge(exped, n - 1)
                for c in range(2):
                    mm = nc.tensor.matmul(sc_bank[n % 2][:, c * D:(c + 1) * D], kst[0:KT, s, h, c * P:(c + 1) * P],
                                          qst[0:KT, s, h, :], start=True, stop=True)
                mm.then_inc(shifted, 1)

            def weigh_values(g):
                b, u = divmod(g, 2)
                pe.wait_ge(exped, 4 * g + 4)
                if u == 0 and b >= 1:
                    pe.wait_ge(o_lo, b)
                for c in range(2):
                    for j in range(4):
                        mm = nc.tensor.matmul(O[32 * j:32 * j + 32, u * D:(u + 1) * D],
                                              vext[:, b % NV, c, 4 * u + j, :], pt[:, g % 2, j, c * D:(c + 1) * D],
                                              start=(c == 0), stop=(c == 1), skip_group_check=True)
                mm.then_inc(valued, 1)

            def place(b):
                pe.wait_ge(o_lo, b + 1)
                if b >= 1:
                    pe.wait_ge(rough, b)
                for w in range(2):
                    for g in range(2):
                        for k, part in enumerate((ohi, olo)):
                            mm = nc.tensor.matmul(R[:, w * D:(w + 1) * D],
                                                  selr[:, (2 * w + g) * P:(2 * w + g + 1) * P],
                                                  part[:, b % 2, g * D:(g + 1) * D],
                                                  start=(g == 0 and k == 0), stop=(g == 1 and k == 1))
                mm.then_inc(placed, 1)

            def turn_tokens(b):
                pe.wait_ge(x2_made, b + 1)
                x_free("tokens", b)
                for c in range(DC):
                    mm = nc.tensor.transpose(X[:, c * P:(c + 1) * P], x2[:, b, c * P:(c + 1) * P], ident)
                mm.then_inc(x_turned, 1)

            def w(t, base, width, c, n):
                return t[:, base + c * width:base + c * width + n]

            def shared_up(b):
                pe.wait_ge(x_lo, b + 1)
                if b == 0:
                    pe.wait_ge(exped, NH)
                    pe.wait_ge(maxed, NH)
                    pe.wait_ge(s_lo, 1)
                if b >= 2:
                    pe.wait_ge(h_made, b - 1)
                    pe.wait_ge(lg_copied, b - 1)
                u1, u3 = u1_bank[b % 2][:, 0:F + WG], u3_bank[b % 2][:, 0:F]
                for c in range(DC):
                    for xpart, parts in ((xhi, (shi, slo)), (xlo, (shi,))):
                        for part in parts:
                            a, z = (c == 0 and xpart is xhi and part is shi), (c == DC - 1 and xpart is xlo)
                            nc.tensor.matmul(u1, xpart[:, b, c, :], w(part, S1, F + WG, c, F + WG), start=a, stop=z)
                            mm = nc.tensor.matmul(u3, xpart[:, b, c, :], w(part, S3, F, c, F), start=a, stop=z)
                mm.then_inc(up_done, 1)

            for s in range(NH + LAG + AFTER):
                if s < NH:
                    scores(s)
                b, rest = divmod(s - H - MROW, H)
                if rest == 0 and 0 <= b < B:
                    turn_maxima(b)
                b, rest = divmod(s - VTURN, H)
                if rest == 0 and 0 <= b < B:
                    turn_values(b)
                if 0 <= s - LAG < NH:
                    shifted_scores(s - LAG)
                g, rest = divmod(s - LAG - 3 - VALUE, 4)
                if rest == 0 and 0 <= g < NG:
                    weigh_values(g)
                if s == NH - 1 + LAG + PLACE:
                    shared_up(0)
                if s == NH - 1 + LAG + NORM:
                    shared_up(1)
                for offset, work in ((PLACE, place), (TTURN, turn_tokens)):
                    b, rest = divmod(s - LAG - H + 1 - offset, H)
                    if rest == 0 and 0 <= b < B:
                        work(b)

            for b in range(2, B):
                shared_up(b)

            pe.wait_ge(route, ROUTE["oh"])
            pe.wait_ge(h_made, B)
            pe.wait_ge(lg_copied, B)
            pe.wait_ge(ones_set, 2)
            nc.tensor.matmul(u1_bank[0][:, 0:B * E], trib[:], oh[:].rearrange("p b e -> p (b e)"), start=True,
                             stop=False, skip_group_check=True)
            for b in range(B - 1):
                mm = nc.tensor.matmul(u1_bank[0][:, E * (b + 1):B * E].rearrange("p (b e) -> p b e", e=E),
                                      onesb[:], oh[:, b:b + 1, :].broadcast_to([P, B - 1 - b, E]),
                                      start=False, stop=(b == B - 2), skip_group_check=True)
            mm.then_inc(pos_done, 1)

            def turn_hidden(b):
                if b == 0:
                    pe.wait_ge(hpad_set, 1)
                if b >= 2:
                    pe.wait_ge(h_lo, b - 1)
                for c in range(FC):
                    mm = nc.tensor.transpose(ht_bank[b % 2][:, c * P:(c + 1) * P], hs[:, b, c * P:(c + 1) * P], ident)
                mm.then_inc(h_turned, 1)

            def shared_down(b):
                pe.wait_ge(h_lo, b + 1)
                if b >= 2:
                    pe.wait_ge(shared_added, b - 1)
                k = 0
                for c in range(FC):
                    for hpart, part in ((hThi, shi), (hThi, slo), (hTlo, shi)):
                        mm = nc.tensor.matmul(y_bank[b % 2][:, 0:D], hpart[:, b % 2, c * P:(c + 1) * P],
                                              w(part, S2, D, c, D), start=(k == 0), stop=(k == 3 * FC - 1))
                        k += 1
                mm.then_inc(down_done, 1)

            turn_hidden(0)
            turn_hidden(1)
            for b in range(B):
                shared_down(b)
                if b + 2 < B:
                    turn_hidden(b + 2)

            def turn_rows(e):
                pe.wait_ge(ld_xe[next(i for i, (a, z) in enumerate(LOADS) if a <= e < z)], 16)
                if e < 2:
                    pe.wait_ge(shared_added, B - 1 + e)
                if e >= 4:
                    pe.wait_ge(e_out, e - 3)
                for c in range(DC):
                    mm = nc.tensor.transpose(y_bank[e % 2][:, c * P:(c + 1) * P], xe[:, e, c * P:(c + 1) * P], ident)
                mm.then_inc(xe_turned, 1)

            def expert_up(e):
                pe.wait_ge(xe_copied, e + 1)
                pe.wait_ge(ld_w[e % NW], 16 * 4 * ring_pass(e, NW))
                if e == 0:
                    pe.wait_ge(route, ROUTE["cum"])
                if e >= 2:
                    pe.wait_ge(e_h, e - 1)
                for c in range(DC):
                    lhs = xdT[:, e % 2, c, :]
                    nc.tensor.matmul(u1_bank[e % 2][:, 0:F], lhs, w(wts[e % NW], W1, F, c, F),
                                     start=(c == 0), stop=(c == DC - 1))
                    mm = nc.tensor.matmul(u3_bank[e % 2][:, 0:F], lhs, w(wts[e % NW], W3, F, c, F),
                                          start=(c == 0), stop=(c == DC - 1))
                mm.then_inc(e_up, 1)

            def turn_expert_hidden(e):
                pe.wait_ge(e_h, e + 1)
                if e == 0:
                    pe.wait_ge(hpad_set, 2)
                if e >= 2:
                    pe.wait_ge(eh_copied, e - 1)
                else:
                    pe.wait_ge(h_lo, B)
                for c in range(FC):
                    mm = nc.tensor.transpose(ht_bank[e % 2][:, c * P:(c + 1) * P], he[:, e % 2, c * P:(c + 1) * P],
                                             ident)
                mm.then_inc(eh_turned, 1)

            def expert_down(e):
                pe.wait_ge(eh_copied, e + 1)
                if e + 2 < E:
                    pe.wait_ge(xe_copied, e + 3)
                else:
                    pe.wait_ge(e_out, e - 1)
                for c in range(FC):
                    rows = P if c < 2 else FL
                    mm = nc.tensor.matmul(y_bank[e % 2][:, 0:D], hTe[0:rows, e % 2, c * P:(c + 1) * P],
                                          wts[e % NW][0:rows, W2 + c * D:W2 + (c + 1) * D],
                                          start=(c == 0), stop=(c == FC - 1))
                mm.then_inc(e_down, 1)

            turn_rows(0)
            for e in range(E + 2):
                if e < E:
                    expert_up(e)
                if 1 <= e <= E:
                    turn_expert_hidden(e - 1)
                if e + 1 < E:
                    turn_rows(e + 1)
                if e >= 2:
                    expert_down(e - 2)


def kernel(x, ctx_2048, itok_B_779_1933, L0_ffn_Wg, L0_ffn_W1, L0_ffn_W3, L0_ffn_W2, L0_ffn_sw1, L0_ffn_sw3,
           L0_ffn_sw2):
    import concourse.bacc as bacc
    from concourse.bass_utils import run_bass_kernel_spmd

    given = {
        "x": x, "ctx": ctx_2048, "lens": itok_B_779_1933, "wg": L0_ffn_Wg, "w1": L0_ffn_W1, "w3": L0_ffn_W3,
        "w2": L0_ffn_W2, "sw1": L0_ffn_sw1, "sw3": L0_ffn_sw3, "sw2": L0_ffn_sw2, "consts": constants(),
    }
    nc = bacc.Bacc("TRN2", target_bir_lowering=False, num_devices=1)
    arrays, args = {}, []
    for name, a in given.items():
        a = np.ascontiguousarray(a)
        arrays[f"in_{name}"] = a
        args.append(nc.dram_tensor(f"in_{name}", a.shape, mybir.dt.from_np(a.dtype), kind="ExternalInput").ap())
    out = nc.dram_tensor("out", (B, P, D), F32, kind="ExternalOutput").ap()
    block_kernel(nc, *args, out)
    r = run_bass_kernel_spmd(nc, [arrays], core_ids=[0])
    return r.results[0]["out"]
```
